# Optimizing a Trainium2 kernel written in Bass

```python
import numpy as np
import jax
import jax.numpy as jnp

def _softmax(x, axis=-1):
    return jax.nn.softmax(x, axis=axis)

def _gelu(x):
    return jax.nn.gelu(x, approximate=True)

def _silu(x):
    return jax.nn.silu(x)

def _sigmoid(x):
    return jax.nn.sigmoid(x)

def _layernorm(x, axis=-1, eps=1e-05):
    m = jnp.mean(x, axis=axis, keepdims=True)
    v = jnp.var(x, axis=axis, keepdims=True)
    return (x - m) / jnp.sqrt(v + eps)

def _scatter_add(tgt, idx, src, axis=0):
    return tgt.at[idx].add(src)

def _segment_sum(src, seg, n):
    return jax.ops.segment_sum(src, seg, n)
kernel_name = 'mk_seq_postln_d2_jaxref_r8_f2ff0c'

def setup_inputs(seed: int=0):
    np.random.seed(seed)
    _w = jnp.asarray

    def _L0_attn_setup():
        import jax, jax.numpy as jnp
        import numpy as np
        B, S, D, H = (2, 256, 128, 16)
        HD = D // H
        key = jax.random.key(seed)
        ks = jax.random.split(key, 5)
        scale = 0.02
        x = jax.random.normal(ks[0], (B, S, D), dtype=jnp.float32)
        Wq = jax.random.normal(ks[1], (D, D), dtype=jnp.float32) * scale
        Wk = jax.random.normal(ks[2], (D, D), dtype=jnp.float32) * scale
        Wv = jax.random.normal(ks[3], (D, D), dtype=jnp.float32) * scale
        Wo = jax.random.normal(ks[4], (D, D), dtype=jnp.float32) * scale
        z = jnp.zeros((D,), dtype=jnp.float32)
        return {'x': x, 'Wq': Wq, 'bq': z, 'Wk': Wk, 'bk': z, 'Wv': Wv, 'bv': z, 'Wo': Wo, 'bo': z}
    _L0_attn_in = _L0_attn_setup()

    def _L0_ffn_setup():
        import jax, jax.numpy as jnp
        import numpy as np
        HIDDEN = 128
        NUM_EXPERTS = 8
        TOP_K = 2
        B, S = (4, 128)
        key = jax.random.key(seed)
        ks = jax.random.split(key, 8)
        H, E = (HIDDEN, NUM_EXPERTS)
        sc = lambda fan_in: 1.0 / np.sqrt(fan_in)
        x = jax.random.normal(ks[0], (B, S, H), dtype=jnp.float32)
        Wr = jax.random.uniform(ks[1], (H, E), minval=-sc(H), maxval=sc(H), dtype=jnp.float32)
        br = jax.random.uniform(ks[2], (E,), minval=-sc(H), maxval=sc(H), dtype=jnp.float32)
        W1 = jax.random.uniform(ks[3], (E, H, 2 * H), minval=-sc(H), maxval=sc(H), dtype=jnp.float32)
        b1 = jax.random.uniform(ks[4], (E, 2 * H), minval=-sc(H), maxval=sc(H), dtype=jnp.float32)
        W2 = jax.random.uniform(ks[5], (E, 2 * H, H), minval=-sc(2 * H), maxval=sc(2 * H), dtype=jnp.float32)
        b2 = jax.random.uniform(ks[6], (E, H), minval=-sc(2 * H), maxval=sc(2 * H), dtype=jnp.float32)
        return {'x': x, 'Wr': Wr, 'br': br, 'W1': W1, 'b1': b1, 'W2': W2, 'b2': b2}
    _L0_ffn_in = _L0_ffn_setup()

    def _L1_attn_setup():
        import jax, jax.numpy as jnp
        import numpy as np
        B, T, D, H, R = (1, 512, 128, 16, 64)
        HD = D // H
        STD = 0.02

        def _low_rank_proj(x, a, b):
            mid = jnp.einsum('btd,hdr->bhtr', x, a)
            return jnp.einsum('bhtr,hrd->bhtd', mid, b)
        key = jax.random.key(seed)
        ks = jax.random.split(key, 8)
        return {'hidden_states': jax.random.normal(ks[0], (B, T, D), jnp.float32), 'q_a': STD * jax.random.normal(ks[1], (H, D, R), jnp.float32), 'q_b': STD * jax.random.normal(ks[2], (H, R, HD), jnp.float32), 'k_a': STD * jax.random.normal(ks[3], (H, D, R), jnp.float32), 'k_b': STD * jax.random.normal(ks[4], (H, R, HD), jnp.float32), 'v_w': STD * jax.random.normal(ks[5], (D, D), jnp.float32), 'v_b': jnp.zeros((D,), jnp.float32), 'o_w': STD * jax.random.normal(ks[6], (D, D), jnp.float32), 'o_b': jnp.zeros((D,), jnp.float32)}
    _L1_attn_in = _L1_attn_setup()

    def _L1_ffn_setup():
        import jax, jax.numpy as jnp
        import numpy as np
        import math
        D = 128
        H = 16
        E = 8
        TOPK = 2
        LAT = D // 2
        KPH = LAT // H
        HD = D // H

        def _forward(hs, q_w, q_b, k_w, k_b, v_w, v_b, o_w, o_b, router_w, router_b, w1, b1, w2, b2):
            B, S, _ = hs.shape
            Q = (hs @ q_w + q_b).reshape(B, S, H, HD).transpose(0, 2, 1, 3)
            K = (hs @ k_w + k_b).reshape(B, S, H, KPH).transpose(0, 2, 1, 3)
            V = (hs @ v_w + v_b).reshape(B, S, H, KPH).transpose(0, 2, 1, 3)
            scores = jnp.einsum('bhsk,bhtk->bhst', Q[..., :KPH], K) / math.sqrt(KPH)
            attn = jax.nn.softmax(scores, axis=-1)
            ao = jnp.einsum('bhst,bhtv->bhsv', attn, V)
            ao = ao.transpose(0, 2, 1, 3).reshape(B, S, H * KPH)
            ao = jnp.concatenate([ao, jnp.zeros((B, S, D - LAT), ao.dtype)], axis=-1)
            mla_out = ao @ o_w + o_b
            probs = jax.nn.softmax(mla_out @ router_w + router_b, axis=-1)
            topw, topi = jax.lax.top_k(probs, TOPK)
            topw = topw / (topw.sum(-1, keepdims=True) + 1e-08)
            combine = jnp.sum(jax.nn.one_hot(topi, E, dtype=probs.dtype) * topw[..., None], axis=-2)
            h1 = jnp.einsum('bsd,edf->ebsf', mla_out, w1) + b1[:, None, None, :]
            h1 = jax.nn.gelu(h1, approximate=False)
            h2 = jnp.einsum('ebsf,efd->ebsd', h1, w2) + b2[:, None, None, :]
            moe_out = jnp.einsum('bse,ebsd->bsd', combine, h2)
            return hs + 0.3 * moe_out
        key = jax.random.key(seed)
        ks = jax.random.split(key, 16)
        s = 0.02
        inp = {'hidden_states': jax.random.normal(ks[0], (2, 256, D), jnp.float32), 'q_w': jax.random.normal(ks[1], (D, D), jnp.float32) * s, 'q_b': jnp.zeros((D,), jnp.float32), 'k_w': jax.random.normal(ks[2], (D, LAT), jnp.float32) * s, 'k_b': jnp.zeros((LAT,), jnp.float32), 'v_w': jax.random.normal(ks[3], (D, LAT), jnp.float32) * s, 'v_b': jnp.zeros((LAT,), jnp.float32), 'o_w': jax.random.normal(ks[4], (D, D), jnp.float32) * s, 'o_b': jnp.zeros((D,), jnp.float32), 'router_w': jax.random.normal(ks[5], (D, E), jnp.float32) * s, 'router_b': jnp.zeros((E,), jnp.float32), 'w1': jax.random.normal(ks[6], (E, D, 2 * D), jnp.float32) * s, 'b1': jnp.zeros((E, 2 * D), jnp.float32), 'w2': jax.random.normal(ks[7], (E, 2 * D, D), jnp.float32) * s, 'b2': jnp.zeros((E, D), jnp.float32)}
        return inp
    _L1_ffn_in = _L1_ffn_setup()
    _d = {'L0_attn_x': _L0_attn_in['x'], 'L0_attn_Wq': _L0_attn_in['Wq'], 'L0_attn_bq': _L0_attn_in['bq'], 'L0_attn_Wk': _L0_attn_in['Wk'], 'L0_attn_bk': _L0_attn_in['bk'], 'L0_attn_Wv': _L0_attn_in['Wv'], 'L0_attn_bv': _L0_attn_in['bv'], 'L0_attn_Wo': _L0_attn_in['Wo'], 'L0_attn_bo': _L0_attn_in['bo'], 'L0_ffn_Wr': _L0_ffn_in['Wr'], 'L0_ffn_br': _L0_ffn_in['br'], 'L0_ffn_W1': _L0_ffn_in['W1'], 'L0_ffn_b1': _L0_ffn_in['b1'], 'L0_ffn_W2': _L0_ffn_in['W2'], 'L0_ffn_b2': _L0_ffn_in['b2'], 'L1_attn_q_a': _L1_attn_in['q_a'], 'L1_attn_q_b': _L1_attn_in['q_b'], 'L1_attn_k_a': _L1_attn_in['k_a'], 'L1_attn_k_b': _L1_attn_in['k_b'], 'L1_attn_v_w': _L1_attn_in['v_w'], 'L1_attn_v_b': _L1_attn_in['v_b'], 'L1_attn_o_w': _L1_attn_in['o_w'], 'L1_attn_o_b': _L1_attn_in['o_b'], 'L1_ffn_q_w': _L1_ffn_in['q_w'], 'L1_ffn_q_b': _L1_ffn_in['q_b'], 'L1_ffn_k_w': _L1_ffn_in['k_w'], 'L1_ffn_k_b': _L1_ffn_in['k_b'], 'L1_ffn_v_w': _L1_ffn_in['v_w'], 'L1_ffn_v_b': _L1_ffn_in['v_b'], 'L1_ffn_o_w': _L1_ffn_in['o_w'], 'L1_ffn_o_b': _L1_ffn_in['o_b'], 'L1_ffn_router_w': _L1_ffn_in['router_w'], 'L1_ffn_router_b': _L1_ffn_in['router_b'], 'L1_ffn_w1': _L1_ffn_in['w1'], 'L1_ffn_b1': _L1_ffn_in['b1'], 'L1_ffn_w2': _L1_ffn_in['w2'], 'L1_ffn_b2': _L1_ffn_in['b2']}
    _x0 = _d['L0_attn_x']
    _d['L0_attn_x'] = jax.random.normal(jax.random.fold_in(jax.random.key(seed), 1), (2, 1024, 128), dtype=_x0.dtype)
    del _x0
    return _d

def reference(L0_attn_x, L0_attn_Wq, L0_attn_bq, L0_attn_Wk, L0_attn_bk, L0_attn_Wv, L0_attn_bv, L0_attn_Wo, L0_attn_bo, L0_ffn_Wr, L0_ffn_br, L0_ffn_W1, L0_ffn_b1, L0_ffn_W2, L0_ffn_b2, L1_attn_q_a, L1_attn_q_b, L1_attn_k_a, L1_attn_k_b, L1_attn_v_w, L1_attn_v_b, L1_attn_o_w, L1_attn_o_b, L1_ffn_q_w, L1_ffn_q_b, L1_ffn_k_w, L1_ffn_k_b, L1_ffn_v_w, L1_ffn_v_b, L1_ffn_o_w, L1_ffn_o_b, L1_ffn_router_w, L1_ffn_router_b, L1_ffn_w1, L1_ffn_b1, L1_ffn_w2, L1_ffn_b2):

    def _L0_attn_ref(x, Wq, bq, Wk, bk, Wv, bv, Wo, bo):
        import jax, jax.numpy as jnp
        import numpy as np
        B, S, D, H = (2, 256, 128, 16)
        HD = D // H
        b, s, d = x.shape
        hd = d // H

        def heads(W, bias):
            return (x @ W.T + bias).reshape(b, s, H, hd).transpose(0, 2, 1, 3)
        q = heads(Wq, bq)
        k = heads(Wk, bk)
        v = heads(Wv, bv)
        scale = 1.0 / np.sqrt(hd).astype(np.float32)
        attn = scale * jnp.einsum('bhqd,bhkd->bhqk', q, k)
        causal = jnp.tril(jnp.ones((s, s), dtype=bool))
        attn = jnp.where(causal[None, None], attn, -jnp.inf)
        attn = jax.nn.softmax(attn, axis=-1)
        ans = jnp.einsum('bhqk,bhkd->bhqd', attn, v)
        ans = ans.transpose(0, 2, 1, 3).reshape(b, s, d)
        return ans @ Wo.T + bo

    def _L0_ffn_ref(x, Wr, br, W1, b1, W2, b2):
        import jax, jax.numpy as jnp
        import numpy as np
        HIDDEN = 128
        NUM_EXPERTS = 8
        TOP_K = 2
        B, S = (4, 128)
        B_, S_, H = x.shape
        xf = x.reshape(-1, H)
        logits = xf @ Wr + br
        topk_w, topk_idx = jax.lax.top_k(logits, TOP_K)
        topk_w = jax.nn.softmax(topk_w, axis=-1)
        gate = jnp.sum(jax.nn.one_hot(topk_idx, NUM_EXPERTS, dtype=xf.dtype) * topk_w[..., None], axis=1)
        h = jax.nn.relu(jnp.einsum('th,ehf->etf', xf, W1) + b1[:, None, :])
        y = jnp.einsum('etf,efh->eth', h, W2) + b2[:, None, :]
        out = jnp.einsum('te,eth->th', gate, y)
        return out.reshape(B_, S_, H)

    def _L1_attn_ref(hidden_states, q_a, q_b, k_a, k_b, v_w, v_b, o_w, o_b):
        import jax, jax.numpy as jnp
        import numpy as np
        B, T, D, H, R = (1, 512, 128, 16, 64)
        HD = D // H
        STD = 0.02

        def _low_rank_proj(x, a, b):
            mid = jnp.einsum('btd,hdr->bhtr', x, a)
            return jnp.einsum('bhtr,hrd->bhtd', mid, b)
        Bc, Tc, Dc = hidden_states.shape
        q = _low_rank_proj(hidden_states, q_a, q_b)
        k = _low_rank_proj(hidden_states, k_a, k_b)
        v = hidden_states @ v_w.T + v_b
        v = v.reshape(Bc, Tc, H, HD).transpose(0, 2, 1, 3)
        scale = 1.0 / np.sqrt(HD).astype(np.float32)
        att = jnp.einsum('bhtd,bhsd->bhts', q, k) * scale
        causal = jnp.tril(jnp.ones((Tc, Tc), dtype=bool))
        att = jnp.where(causal[None, None], att, jnp.finfo(att.dtype).min)
        att = jax.nn.softmax(att, axis=-1)
        y = jnp.einsum('bhts,bhsd->bhtd', att, v)
        y = y.transpose(0, 2, 1, 3).reshape(Bc, Tc, Dc)
        return y @ o_w.T + o_b

    def _L1_ffn_ref(hidden_states, q_w, q_b, k_w, k_b, v_w, v_b, o_w, o_b, router_w, router_b, w1, b1, w2, b2):
        import jax, jax.numpy as jnp
        import numpy as np
        import math
        D = 128
        H = 16
        E = 8
        TOPK = 2
        LAT = D // 2
        KPH = LAT // H
        HD = D // H

        def _forward(hs, q_w, q_b, k_w, k_b, v_w, v_b, o_w, o_b, router_w, router_b, w1, b1, w2, b2):
            B, S, _ = hs.shape
            Q = (hs @ q_w + q_b).reshape(B, S, H, HD).transpose(0, 2, 1, 3)
            K = (hs @ k_w + k_b).reshape(B, S, H, KPH).transpose(0, 2, 1, 3)
            V = (hs @ v_w + v_b).reshape(B, S, H, KPH).transpose(0, 2, 1, 3)
            scores = jnp.einsum('bhsk,bhtk->bhst', Q[..., :KPH], K) / math.sqrt(KPH)
            attn = jax.nn.softmax(scores, axis=-1)
            ao = jnp.einsum('bhst,bhtv->bhsv', attn, V)
            ao = ao.transpose(0, 2, 1, 3).reshape(B, S, H * KPH)
            ao = jnp.concatenate([ao, jnp.zeros((B, S, D - LAT), ao.dtype)], axis=-1)
            mla_out = ao @ o_w + o_b
            probs = jax.nn.softmax(mla_out @ router_w + router_b, axis=-1)
            topw, topi = jax.lax.top_k(probs, TOPK)
            topw = topw / (topw.sum(-1, keepdims=True) + 1e-08)
            combine = jnp.sum(jax.nn.one_hot(topi, E, dtype=probs.dtype) * topw[..., None], axis=-2)
            h1 = jnp.einsum('bsd,edf->ebsf', mla_out, w1) + b1[:, None, None, :]
            h1 = jax.nn.gelu(h1, approximate=False)
            h2 = jnp.einsum('ebsf,efd->ebsd', h1, w2) + b2[:, None, None, :]
            moe_out = jnp.einsum('bse,ebsd->bsd', combine, h2)
            return hs + 0.3 * moe_out
        return _forward(hidden_states, q_w, q_b, k_w, k_b, v_w, v_b, o_w, o_b, router_w, router_b, w1, b1, w2, b2)
    x = L0_attn_x
    x = _layernorm(x + _L0_attn_ref(x, L0_attn_Wq, L0_attn_bq, L0_attn_Wk, L0_attn_bk, L0_attn_Wv, L0_attn_bv, L0_attn_Wo, L0_attn_bo), axis=-1)
    x = _layernorm(x + _L0_ffn_ref(x, L0_ffn_Wr, L0_ffn_br, L0_ffn_W1, L0_ffn_b1, L0_ffn_W2, L0_ffn_b2), axis=-1)
    x = _layernorm(x + _L1_attn_ref(x, L1_attn_q_a, L1_attn_q_b, L1_attn_k_a, L1_attn_k_b, L1_attn_v_w, L1_attn_v_b, L1_attn_o_w, L1_attn_o_b), axis=-1)
    x = _layernorm(x + _L1_ffn_ref(x, L1_ffn_q_w, L1_ffn_q_b, L1_ffn_k_w, L1_ffn_k_b, L1_ffn_v_w, L1_ffn_v_b, L1_ffn_o_w, L1_ffn_o_b, L1_ffn_router_w, L1_ffn_router_b, L1_ffn_w1, L1_ffn_b1, L1_ffn_w2, L1_ffn_b2), axis=-1)
    return x

_drawn_inputs = setup_inputs


def setup_inputs(seed=0):
    import zlib

    import numpy as np

    out = dict(_drawn_inputs(seed))
    spreads = {'L0_attn_bq': (0.0, 0.8),
     'L0_attn_bk': (0.0, 0.8),
     'L0_attn_bv': (0.0, 0.291),
     'L0_attn_bo': (0.0, 0.1),
     'L1_attn_v_b': (0.0, 0.351),
     'L1_attn_o_b': (0.0, 0.1),
     'L1_ffn_q_b': (0.0, 0.8),
     'L1_ffn_k_b': (0.0, 0.8),
     'L1_ffn_v_b': (0.0, 0.8),
     'L1_ffn_o_b': (0.0, 0.8),
     'L1_ffn_router_b': (0.0, 0.727),
     'L1_ffn_b1': (0.0, 0.8),
     'L1_ffn_b2': (0.0, 0.733)}
    factors = {'L0_attn_Wq': 8.0,
     'L0_attn_Wk': 8.0,
     'L0_attn_Wv': 6.502,
     'L0_ffn_b1': 3.936,
     'L1_attn_q_a': 8.0,
     'L1_attn_q_b': 8.0,
     'L1_attn_k_a': 8.0,
     'L1_attn_k_b': 8.0,
     'L1_attn_v_w': 7.561,
     'L1_ffn_q_w': 8.0,
     'L1_ffn_k_w': 8.0,
     'L1_ffn_v_w': 8.0,
     'L1_ffn_o_w': 8.0,
     'L1_ffn_router_w': 8.0,
     'L1_ffn_w1': 8.0,
     'L1_ffn_w2': 8.0}
    for name, (base, spread) in spreads.items():
        noise = np.random.default_rng([zlib.crc32(name.encode()), seed]).standard_normal(out[name].shape)
        drawn = base * np.exp(spread * noise) if base else spread * noise
        out[name] = jnp.asarray(drawn.astype(out[name].dtype))
    for name, factor in factors.items():
        out[name] = (out[name] * factor).astype(out[name].dtype)
    return out
```

```python
from contextlib import ExitStack

import concourse.bass as bass
from concourse import mybir

ALU = mybir.AluOpType
ACT = mybir.ActivationFunctionType
AX = mybir.AxisListType
F32 = mybir.dt.float32
BF16 = mybir.dt.bfloat16
U32 = mybir.dt.uint32
I32 = mybir.dt.int32

P = 128
B, S, D = 2, 1024, 128
T = B * S
NT = T // P
TB = S // P
H = 16
NH = B * H
E = 8
F = 2 * D
FB = F // P
CH = 512
NCH = T // CH
TPC = CH // P
PARTS = 3
RING = 4
AHEAD = 2
Q = 32
LOWEST = -3.0e38
LN_EPS = 1e-5
RANK = 64
MIX = 0.3


class Attention:

    def __init__(self, layer, head_dim, scale_dim, causal):
        self.layer = layer
        self.hd = head_dim
        self.width = H * head_dim
        self.rows = PARTS * PARTS * head_dim
        self.rows_m = self.rows + PARTS
        self.dv = head_dim + 1
        self.scale = float(scale_dim) ** -0.5
        self.causal = causal
        if causal:
            diagonal = [[(i, i, 1) for i in range(4 * c, 4 * c + 4)] for c in range(2)]
            self.by_query = diagonal + [
                [(7, 0, 4)], [(7, 4, 3), (1, 0, 1)], [(6, 0, 4)], [(6, 4, 2), (2, 0, 2)],
                [(5, 0, 4)], [(5, 4, 1), (3, 0, 3)], [(4, 0, 4)]]
            self.maxima = 3
            self.by_key = [
                [(i, i, 1, 3) for i in range(4)], [(0, 4, 4, 0)], [(1, 4, 4, 1)],
                [(0, 1, 3, 3), (2, 3, 1, 3)], [(2, 4, 4, 2)], [(3, 4, 4, 0)],
                [(4, 4, 1, 1), (5, 5, 1, 2), (6, 6, 1, 1), (7, 7, 1, 2)], [(1, 2, 2, 3), (5, 6, 2, 0)],
                [(4, 5, 3, 1), (6, 7, 1, 2)]]
            self.masked = (0, 6)
            self.batch = 3
            self.quarters = ((96, 128), (0, 96))
        else:
            self.by_query = [[(i, 4 * c, 4)] for i in range(TB) for c in range(2)]
            self.maxima = 2
            self.by_key = [[(j, 4 * half, 4, j % 4)] for four in (0, 4) for half in range(2)
                           for j in range(four, four + 4)]
            self.masked = ()
            self.batch = 4
            self.quarters = ((0, 128), (0, 128))
        self.chunks = len(self.by_key)
        self.batches = [range(c, c + self.batch) for c in range(0, self.chunks, self.batch)]
        self.probs_ring = 2 * self.batch

    def query_diagonal(self, c):
        return self.causal and c < 2


ATTENTIONS = [Attention(0, 8, 8, True), Attention(1, 8, 8, True), Attention(2, 4, 4, False)]


def build(nc, inp, out):
    ctx = ExitStack()
    with ctx:
        def sb(name, shape, dt=F32):
            return ctx.enter_context(nc.sbuf_tensor(name, shape, dt))

        sems = {}

        def sem(name):
            if name not in sems:
                sems[name] = ctx.enter_context(nc.semaphore(name))
            return sems[name]

        qk_dram = [[nc.dram_tensor(f"{w}_parts_{a.layer}", (PARTS, B, a.width, S), BF16, kind="Internal").ap()
                    for w in "qk"] for a in ATTENTIONS]

        x = sb("x", [P, NT, D])
        xT = sb("xT", [P, T])
        x_plus = sb("x_plus", [P, NT, D])
        acc = sb("acc", [P, NT, D])
        parts = [sb("q_parts", [P, PARTS, T], BF16), sb("k_parts", [P, PARTS, T], BF16)]
        whole = sb("whole", [P, 2, CH])
        rest = sb("rest", [P, 2, CH])
        qx = sb("qx", [P, RING, S], BF16)
        kx = sb("kx", [P, RING, S], BF16)
        kx4 = sb("kx4", [P, RING, S], BF16)
        v_all = [sb("v8", [P, NH, TB, 9]), sb("v4", [P, NH, TB, 5])]
        v_head = sb("v_head", [P, RING, TB, Q])
        probs = sb("probs", [P, 8, CH])
        sums = sb("sums", [P, 2, 2, CH])
        by_quarter = sb("by_quarter", [P, 2, TB, 4, 9])
        pairs = sb("pairs", [P, TB, 2, 9])
        total = sb("total", [P, 2, TB, 9])
        tile_max = sb("tile_max", [P, RING, TB, 3])
        neg_max = sb("neg_max", [P, RING, TB])
        neg_rest = sb("neg_rest", [P, 2, TB])
        neg_parts = sb("neg_parts", [P, RING, PARTS, TB], BF16)
        neg_rows = sb("neg_rows", [PARTS * TB, RING, P], BF16)
        den_inv = sb("den_inv", [P, 2, TB])
        heads_out = sb("heads_out", [P, NH * TB * 8])
        a_tok = sb("a_tok", [P, NT, D])
        aT = sb("aT", [P, T])
        hidden = probs[:, 0:4, :].rearrange("p (m f) c -> p m f c", f=FB)
        stats = sb("stats", [P, NT, 6])
        mean_var = sb("mean_var", [P, NT, 2])
        std = sb("std", [P, NT])
        rstd = sb("rstd", [P, NT])
        logits = sb("logits", [P, NT, E])
        top = sb("top", [P, NT, E])
        top_at = sb("top_at", [P, NT, E], U32)
        top_f = sb("top_f", [P, NT, 2])
        small = sb("small", [P, 6, NT])
        pick = sb("pick", [P, 2, NT, E])
        gate = sb("gate", [P, NT, E])
        gateT = aT[0:E, :]
        iota_i = sb("iota_i", [P, E], I32)
        iota = sb("iota", [P, E])
        ident = sb("ident", [P, P])
        ident16 = sb("ident16", [P, P], BF16)
        mask16 = sb("mask16", [P, 4, P], BF16)
        w_sb = {n: sb("sb_" + n, list(ap.shape)) for n, (ap, _) in inp.items()
                if n not in ("x", "q_aT", "k_aT")}
        w_sb["q_aT"] = acc[0:RANK]
        w_sb["k_aT"] = a_tok[0:RANK]
        w_eff = [sb("wq_eff", [P, D]), sb("wk_eff", [P, D])]

        bank = [ctx.enter_context(nc.psum_tensor(f"bank{i}", [P, CH], F32)) for i in range(8)]
        S1 = bank[0:2]
        S2 = bank[2:4]
        SUM = bank[4:6]
        OUT = bank[6:8]
        neg_ps = bank[7][0:PARTS * TB, 0:P // 2].bitcast(BF16)

        def kx_of(a):
            return kx if a.hd == 8 else kx4

        def v_of(a):
            return v_all[0 if a.hd == 8 else 1]

        groups = {}
        for n, (ap, g) in inp.items():
            if n != "x":
                groups.setdefault(g, []).append(n)

        def loaded(eng, g):
            eng.wait_ge(sem(f"loaded_{g}"), 16 * len(groups[g]))

        def ge(eng, name, value):
            if isinstance(value, int) and value <= 0:
                return
            eng.wait_ge(sem(name), value)

        def qkv_weights(a):
            if a.layer == 0:
                return w_sb["wqT0"][:], w_sb["wkT0"][:], w_sb["wvT0"][:], w_sb["bv0"], w_sb["bq0"], w_sb["bk0"]
            if a.layer == 1:
                return w_eff[0][:], w_eff[1][:], w_sb["wvT1"][:], w_sb["bv1"], None, None
            return w_sb["wq2"][:], w_sb["wk2"][:], w_sb["wv2"][:], w_sb["bv2"], w_sb["bq2"], w_sb["bk2"]

        block = ctx.enter_context(nc.Block())

        def over_heads(eng, head):
            for slot in range(RING):
                head(0, slot)
            with eng.Fori(1, NH // RING - 1) as turn:
                for slot in range(RING):
                    head(turn, slot)
            for slot in range(RING):
                head(NH // RING - 1, slot)

        def turns_before(layer):
            return layer * (NH // RING)

        def is_first(n):
            return isinstance(n, int) and n == 0

        def is_last(turn, slot, ahead):
            return isinstance(turn, int) and RING * turn + slot + ahead >= NH

        @block.sync
        def _(sp):
            for c in range(NCH):
                sp.dma_start(x[:, TPC * c:TPC * (c + 1), :],
                             inp["x"][0].rearrange("(t p) d -> p t d", p=P)[:, TPC * c:TPC * (c + 1), :]
                             ).then_inc(sem("loaded_x"), 16)
            for g in groups:
                for n in groups[g]:
                    sp.dma_start(w_sb[n][:], inp[n][0]).then_inc(sem(f"loaded_{g}"), 16)

            def attention(a):
                L = a.layer
                C = a.chunks

                def store_parts(b):
                    for w in range(2):
                        sp.wait_ge(sem(f"part3_{L}"), (2 * b + w + 1) * (NCH // B))
                        for p in range(PARTS):
                            sp.dma_start(qk_dram[L][w][p, b], parts[w][0:a.width, p, S * b:S * (b + 1)]
                                         ).then_inc(sem(f"parts_out{b}_{L}"), 16)
                    sp.wait_ge(sem(f"parts_out{b}_{L}"), 16 * 2 * PARTS)

                def by_head(w):
                    return qk_dram[L][w].rearrange("c b (h d) t -> c (b h) d t", d=a.hd)

                def load_head(turn, slot):
                    n = RING * turn + slot
                    rows = PARTS * a.hd
                    for i in range(PARTS):
                        q = by_head(0)[i:i + 1, bass.ds(n, 1)].rearrange("c n d t -> (c n) d t").to_broadcast([PARTS, a.hd, S])
                        sp.dma_start(qx[rows * i:rows * (i + 1), slot, :], q).then_inc(sem(f"qk_in{slot}"), 16)
                        k = by_head(1)[:, bass.ds(n, 1)].rearrange("c n d t -> (c n) d t")
                        sp.dma_start(kx_of(a)[rows * i:rows * (i + 1), slot, :], k).then_inc(sem(f"qk_in{slot}"), 16)

                def load_max(turn, slot):
                    for p in range(PARTS):
                        sp.dma_start(qx[a.rows + p:a.rows + p + 1, slot, :],
                                     neg_rows[TB * p:TB * (p + 1), slot, :]).then_inc(sem(f"max_in{slot}"), 16)

                if L == 0:
                    sp.wait_ge(sem("constants"), CONSTANTS)
                store_parts(0)
                for n in range(AHEAD + 1):
                    load_head(0, n)
                store_parts(1)
                ge(sp, f"neg_rows_{L}", 1)
                load_max(0, 0)

                def head(turn, slot):
                    n = RING * turn + slot
                    if not is_last(turn, slot, 3):
                        ge(sp, f"scores_k_{L}", C * n)
                        load_head(turn + (slot + 3) // RING, (slot + 3) % RING)
                    if not is_last(turn, slot, 1):
                        ge(sp, f"neg_rows_{L}", n + 2)
                        load_max(turn + (slot + 1) // RING, (slot + 1) % RING)

                over_heads(sp, head)

            for a in ATTENTIONS:
                attention(a)
            for c in range(NCH):
                sp.wait_ge(sem("normed_4"), c + 1)
                sp.dma_start(out.rearrange("(t p) d -> p t d", p=P)[:, TPC * c:TPC * (c + 1), :],
                             x[:, TPC * c:TPC * (c + 1), :]).then_inc(sem("stored"), 16)
            sp.wait_ge(sem("stored"), 16 * NCH)

        @block.gpsimd
        def _(pool):
            made = [0]

            def constant(ins):
                made[0] += 1
                ins.then_inc(sem("constants"), 1)

            constant(nc.gpsimd.memset(ident[:], 0.0))
            constant(nc.gpsimd.memset(ident16[:], 0.0))
            constant(nc.gpsimd.memset(mask16[:], 0.0))
            pool.wait_ge(sem("constants"), made[0])
            for m in (ident, ident16):
                constant(nc.gpsimd.affine_select(out=m[:], in_=m[:], compare_op=ALU.not_equal, fill=1.0, base=0,
                                                 pattern=[[-1, P]], channel_multiplier=1))
            constant(nc.gpsimd.affine_select(out=mask16[:], in_=mask16[:], compare_op=ALU.is_ge, fill=LOWEST, base=0,
                                             pattern=[[0, 4], [-1, P]], channel_multiplier=1))
            constant(nc.gpsimd.memset(tile_max[:], LOWEST))
            constant(nc.gpsimd.memset(kx[:], 1.0))
            constant(nc.gpsimd.memset(kx4[:], 1.0))
            for v in v_all:
                constant(nc.gpsimd.memset(v[:, :, :, 0:1], 1.0))
            constant(nc.gpsimd.memset(v_head[:], 0.0))
            constant(nc.gpsimd.memset(sums[:], 0.0))
            constant(nc.gpsimd.iota(iota_i[:], pattern=[[1, E]], base=0, channel_multiplier=0))
            pool.wait_ge(sem("constants"), made[0])
            constant(nc.gpsimd.tensor_copy(iota[:], iota_i[:]))
            assert made[0] == CONSTANTS

            def add_bias(L):
                loaded(pool, f"attn{L}")
                if L == 0:
                    pool.wait_ge(sem("loaded_x"), 16 * NCH)
                else:
                    pool.wait_ge(sem(f"normed_{2 * L}"), NCH)
                for c in range(NCH):
                    t = slice(TPC * c, TPC * (c + 1))
                    nc.gpsimd.tensor_tensor(x_plus[:, t, :], x[:, t, :],
                                            w_sb[f"bo{L}"][:].unsqueeze(1).to_broadcast([P, TPC, D]), ALU.add
                                            ).then_inc(sem(f"x_plus_{L}"), 1)

            def attention(a):
                L = a.layer
                C = a.chunks

                def apart(name, value):
                    if not isinstance(value, int):
                        value = pool.to_reg(value)
                        pool.wait_ge(sem("constants"), CONSTANTS)
                    ge(pool, name, value)

                def take_v(turn, slot):
                    n = RING * turn + slot
                    ge(pool, f"pv_{L}", C * (n - 3))
                    nc.gpsimd.tensor_copy(v_head[:, slot, :, 0:a.dv],
                                          v_of(a)[:, bass.ds(n, 1), :, :].rearrange("p n t d -> p (n t) d")
                                          ).then_inc(sem(f"v_head_{L}"), 1)

                def split_max(turn, slot):
                    n = RING * turn + slot
                    whole_m, rest_m = neg_max[:, slot, :], neg_rest[:, slot % 2, :]
                    ge(pool, f"neg_ps_{L}", n - 3)
                    apart(f"neg_max_{L}", n + 1)
                    nc.gpsimd.tensor_copy(neg_parts[:, slot, 0, :], whole_m).then_inc(sem(f"neg_parts_{L}"), 1)
                    pool.wait_ge(sem(f"neg_parts_{L}"), 4 * n + 1)
                    nc.gpsimd.tensor_tensor(rest_m, whole_m, neg_parts[:, slot, 0, :], ALU.subtract
                                            ).then_inc(sem(f"neg_parts_{L}"), 1)
                    apart(f"neg_parts_{L}", 4 * n + 2)
                    nc.gpsimd.tensor_copy(neg_parts[:, slot, 1, :], rest_m).then_inc(sem(f"neg_parts_{L}"), 1)
                    pool.wait_ge(sem(f"neg_parts_{L}"), 4 * n + 3)
                    nc.gpsimd.tensor_tensor(neg_parts[:, slot, 2, :], rest_m, neg_parts[:, slot, 1, :], ALU.subtract
                                            ).then_inc(sem(f"neg_parts_{L}"), 1)

                pool.wait_ge(sem(f"v_all_{L}"), NCH)
                for n in range(AHEAD):
                    take_v(0, n)
                for n in range(AHEAD):
                    split_max(0, n)

                def add_quarters(n, parity):
                    q = by_quarter[:, parity, :, :, 0:a.dv]
                    pool.wait_ge(sem(f"by_quarter_{L}"), 2 * (n + 1))
                    ge(pool, f"total_{L}", 2 * n)
                    nc.gpsimd.tensor_tensor(pairs[:, :, :, 0:a.dv], q[:, :, 0:2, :], q[:, :, 2:4, :], ALU.add
                                            ).then_inc(sem(f"total_{L}"), 1)
                    pool.wait_ge(sem(f"total_{L}"), 2 * n + 1)
                    ge(pool, f"normalised_{L}", 2 * (n - 1))
                    nc.gpsimd.tensor_tensor(total[:, parity, :, 0:a.dv], pairs[:, :, 0, 0:a.dv], pairs[:, :, 1, 0:a.dv],
                                            ALU.add).then_inc(sem(f"total_{L}"), 1)

                def mask(turn, slot, which):
                    n = RING * turn + slot
                    c = a.masked[which]
                    p = probs[:, (C * slot + c) % a.probs_ring, :].rearrange("p (t q) -> p t q", q=P)
                    apart(f"probs_{L}", C * n + c + 1)
                    nc.gpsimd.affine_select(out=p, in_=p, compare_op=ALU.is_ge, fill=0.0, base=0,
                                            pattern=[[0, 4], [1, P]], channel_multiplier=-1
                                            ).then_inc(sem(f"masked_{L}"), 1)

                def head(turn, slot):
                    ahead = (turn + (slot + AHEAD) // RING, (slot + AHEAD) % RING)
                    if a.causal:
                        mask(turn, slot, 0)
                    if not is_last(turn, slot, AHEAD):
                        take_v(*ahead)
                    if not is_first(RING * turn + slot):
                        add_quarters(RING * turn + slot - 1, (slot + 1) % 2)
                    if a.causal:
                        mask(turn, slot, 1)
                    if not is_last(turn, slot, AHEAD):
                        split_max(*ahead)

                over_heads(pool, head)
                add_quarters(NH - 1, (NH - 1) % 2)

            def gather_heads(a):
                pool.wait_ge(sem(f"normalised_{a.layer}"), 2 * NH)
                src = heads_out[:, 0:NH * TB * a.hd].rearrange("p (b h t d) -> p b h t d", b=B, h=H, t=TB)
                for t in range(NT):
                    nc.gpsimd.tensor_copy(a_tok[:, t, 0:a.width].rearrange("p (h d) -> p h d", h=H),
                                          src[:, t // TB, :, t % TB, :]).then_inc(sem(f"a_tok_{a.layer}"), 1)

            for a in ATTENTIONS:
                if a.layer < 2:
                    add_bias(a.layer)
                attention(a)
                gather_heads(a)

        @block.scalar
        def _(act):
            def transposed(k):
                for c in range(NCH):
                    act.wait_ge(sem(f"xT_ps_{k}"), c + 1)
                    nc.scalar.activation(xT[:, CH * c:CH * (c + 1)], bank[c % 2][:], ACT.Copy
                                         ).then_inc(sem(f"xT_{k}"), 1)

            def effective_weights():
                for w in range(2):
                    act.wait_ge(sem("w_eff_ps"), w + 1)
                    nc.scalar.activation(w_eff[w][:], bank[6 + w][:, 0:D], ACT.Copy).then_inc(sem("w_eff"), 1)

            def qkv(a):
                L = a.layer
                wd = a.width
                *_, bq, bk = qkv_weights(a)
                items = [(b, w, c) for b in range(B) for w in range(2) for c in range(NCH // B)]

                def second(m):
                    b, w, c = items[m]
                    t = slice(S * b + CH * c, S * b + CH * (c + 1))
                    act.wait_ge(sem(f"rest_{L}"), m + 1)
                    nc.scalar.activation(parts[w][0:wd, 1, t], rest[0:wd, m % 2, :], ACT.Copy
                                         ).then_inc(sem(f"part2_{L}"), 1)

                for m, (b, w, c) in enumerate(items):
                    t = slice(S * b + CH * c, S * b + CH * (c + 1))
                    act.wait_ge(sem(f"qk_ps_{L}"), m + 1)
                    if m >= 2:
                        act.wait_ge(sem(f"rest_{L}"), m - 1)
                    bias = (bq, bk)[w]
                    kw = {} if bias is None else {"bias": bias[0:wd, :]}
                    nc.scalar.activation(whole[0:wd, m % 2, :], bank[2 + m % 2][0:wd, :], ACT.Identity, **kw
                                         ).then_inc(sem(f"part1_{L}"), 1)
                    nc.scalar.activation(parts[w][0:wd, 0, t], bank[2 + m % 2][0:wd, :], ACT.Identity, **kw
                                         ).then_inc(sem(f"part1_{L}"), 1)
                    if m >= 1:
                        second(m - 1)
                second(len(items) - 1)

            def attention(a):
                L = a.layer
                C = a.chunks

                def rows(turn, slot):
                    n = RING * turn + slot
                    act.wait_ge(sem(f"neg_ps_{L}"), n + 1)
                    ge(act, f"max_in{slot}", 16 * PARTS * (turns_before(L) + turn))
                    nc.scalar.activation(neg_rows[:, slot, :], neg_ps, ACT.Copy
                                         ).then_inc(sem(f"neg_rows_{L}"), 1)

                def take_sums(n, parity):
                    act.wait_ge(sem(f"pv_{L}"), C * (n + 1))
                    ge(act, f"out_{L}", n - 1)
                    for half, (lo, hi) in enumerate(a.quarters):
                        nc.scalar.activation(sums[lo:hi, parity, half, :], SUM[half][lo:hi, :], ACT.Copy
                                             ).then_inc(sem(f"sums_{L}"), 1)

                def take_out(n, parity):
                    act.wait_ge(sem(f"out_{L}"), n + 1)
                    ge(act, f"total_{L}", 2 * (n - 1))
                    for half in range(2):
                        nc.scalar.activation(by_quarter[:, parity, 4 * half:4 * half + 4, :, 0:a.dv],
                                             OUT[half][:].rearrange("p (t g c) -> p t g c", t=4, g=4)[:, :, :, 0:a.dv],
                                             ACT.Copy).then_inc(sem(f"by_quarter_{L}"), 1)

                rows(0, 0)

                def head(turn, slot):
                    n = RING * turn + slot
                    for k, batch in enumerate(a.batches):
                        for c in batch:
                            act.wait_ge(sem(f"scores_k_{L}"), C * n + c + 1)
                            ge(act, f"pv_{L}", C * n + c - a.probs_ring + 1)
                            nc.scalar.activation(probs[:, (C * slot + c) % a.probs_ring, :],
                                                 S2[(C * slot + c) % 2][:], ACT.Exp, scale=a.scale
                                                 ).then_inc(sem(f"probs_{L}"), 1)
                        if k == 0 and not is_last(turn, slot, 1):
                            rows(turn + (slot + 1) // RING, (slot + 1) % RING)
                        if k == 0 and not is_first(n):
                            take_sums(n - 1, (slot + 1) % 2)
                        if k == 1 and not is_first(n):
                            take_out(n - 1, (slot + 1) % 2)

                over_heads(act, head)
                take_sums(NH - 1, (NH - 1) % 2)
                take_out(NH - 1, (NH - 1) % 2)

            def projected(a):
                for c in range(NCH):
                    act.wait_ge(sem(f"aT_ps_{a.layer}"), c + 1)
                    nc.scalar.activation(aT[0:a.width, CH * c:CH * (c + 1)], bank[c % 2][0:a.width, :], ACT.Copy
                                         ).then_inc(sem(f"aT_{a.layer}"), 1)

            def mla():
                for c in range(NCH):
                    act.wait_ge(sem("mla_ps"), c + 1)
                    nc.scalar.activation(xT[:, CH * c:CH * (c + 1)], bank[2 + c % 2][:], ACT.Identity,
                                         bias=w_sb["bo2"][:, 0:1]).then_inc(sem("mla"), 1)

            def deviation(k):
                act.wait_ge(sem("var"), k)
                nc.scalar.activation(std[:], std[:], ACT.Sqrt).then_inc(sem("std"), 1)

            def experts(f):
                act.wait_ge(sem(f"route_in_{f}"), 1)
                if f == 0:
                    nc.scalar.activation(small[:, 0, :], small[:, 0, :], ACT.Exp).then_inc(sem(f"route_exp_{f}"), 1)
                else:
                    nc.scalar.activation(logits[:], logits[:], ACT.Exp).then_inc(sem(f"route_exp_{f}"), 1)
                for c in range(NCH):
                    act.wait_ge(sem(f"gateT_ps_{f}"), c + 1)
                    nc.scalar.activation(gateT[:, CH * c:CH * (c + 1)], bank[4 + c][0:E, :], ACT.Copy
                                         ).then_inc(sem(f"gateT_{f}"), 1)
                for m in range(NCH * E):
                    act.wait_ge(sem(f"hid_ps_{f}"), m + 1)
                    if m >= 2:
                        act.wait_ge(sem(f"y_ps_{f}"), m - 1)
                    for fb in range(FB):
                        e = m % E
                        nc.scalar.activation(hidden[:, m % 2, fb, :], bank[2 * (m % 2) + fb][:],
                                             ACT.Relu if f == 0 else ACT.Gelu,
                                             bias=w_sb[f"b1_{f}"][:, FB * e + fb:FB * e + fb + 1]
                                             ).then_inc(sem(f"hid_{f}"), 1)

            effective_weights()
            loaded(act, "attn0")
            transposed(0)
            qkv(ATTENTIONS[0])
            attention(ATTENTIONS[0])
            projected(ATTENTIONS[0])
            deviation(1)
            transposed(1)
            loaded(act, "ffn0")
            experts(0)
            deviation(2)
            transposed(2)
            qkv(ATTENTIONS[1])
            attention(ATTENTIONS[1])
            projected(ATTENTIONS[1])
            deviation(3)
            transposed(3)
            loaded(act, "attn2")
            qkv(ATTENTIONS[2])
            attention(ATTENTIONS[2])
            projected(ATTENTIONS[2])
            mla()
            loaded(act, "ffn1")
            experts(1)
            deviation(4)

        @block.vector
        def _(dve):
            linked = [0]

            def link(ins):
                linked[0] += 1
                ins.then_inc(sem("vector_chain"), 1)
                dve.wait_ge(sem("vector_chain"), linked[0])

            def v_out(a, c):
                L = a.layer
                dve.wait_ge(sem(f"v_ps_{L}"), c + 1)
                bv = qkv_weights(a)[3]
                for t in range(TPC):
                    tile = TPC * c + t
                    ins = nc.vector.tensor_tensor(
                        v_of(a)[:, H * (tile // TB):H * (tile // TB + 1), tile % TB, 1:a.dv],
                        bank[4 + c % 2][:, P * t:P * t + a.width].rearrange("p (h d) -> p h d", h=H),
                        bv[:].rearrange("p (h d) -> p h d", h=H), ALU.add)
                ins.then_inc(sem(f"v_all_{L}"), 1)

            def qkv(a):
                L = a.layer
                wd = a.width
                items = [(b, w, c) for b in range(B) for w in range(2) for c in range(NCH // B)]

                def third(m):
                    b, w, c = items[m]
                    t = slice(S * b + CH * c, S * b + CH * (c + 1))
                    dve.wait_ge(sem(f"part2_{L}"), m + 1)
                    nc.vector.tensor_tensor(parts[w][0:wd, 2, t], rest[0:wd, m % 2, :], parts[w][0:wd, 1, t],
                                            ALU.subtract).then_inc(sem(f"part3_{L}"), 1)

                if L == 0:
                    dve.wait_ge(sem("constants"), CONSTANTS)
                for m, (b, w, c) in enumerate(items):
                    t = slice(S * b + CH * c, S * b + CH * (c + 1))
                    dve.wait_ge(sem(f"part1_{L}"), 2 * m + 2)
                    if m >= 2:
                        dve.wait_ge(sem(f"part3_{L}"), m - 1)
                    nc.vector.tensor_tensor(rest[0:wd, m % 2, :], whole[0:wd, m % 2, :], parts[w][0:wd, 0, t],
                                            ALU.subtract).then_inc(sem(f"rest_{L}"), 1)
                    if m >= 1:
                        third(m - 1)
                    if m % 2 == 1:
                        v_out(a, m // 2)
                third(len(items) - 1)

            def attention(a):
                L = a.layer
                C = a.chunks

                def find_max(turn, slot, c):
                    n = RING * turn + slot
                    s1 = S1[(C * slot + c) % 2]
                    dve.wait_ge(sem(f"scores_q_{L}"), C * n + c + 1)
                    if c == 0:
                        ge(dve, f"neg_max_{L}", n - 3)
                    if a.query_diagonal(c):
                        ins = nc.vector.tensor_reduce(tile_max[:, slot, 4 * c:4 * c + 4, 0],
                                                      s1[:].rearrange("p (t k) -> p t k", k=P), AX.X, ALU.max)
                    else:
                        at = 0
                        for i, first, count in a.by_query[c]:
                            which = (1 if a.causal else 0) + first // 4
                            ins = nc.vector.tensor_reduce(tile_max[:, slot, i, which:which + 1],
                                                          s1[:, at:at + P * count], AX.X, ALU.max)
                            at += P * count
                    ins.then_inc(sem(f"max_taken_{L}"), 1)

                def combine_max(turn, slot):
                    n = RING * turn + slot
                    dve.wait_ge(sem(f"max_taken_{L}"), C * (n + 1))
                    ge(dve, f"neg_parts_{L}", 4 * (n - 3))
                    nc.vector.tensor_reduce(neg_max[:, slot, :], tile_max[:, slot, :, 0:a.maxima], AX.X, ALU.max,
                                            negate=True).then_inc(sem(f"neg_max_{L}"), 1)

                def normalise(n, parity):
                    o = total[:, parity, :, 0:a.dv]
                    dve.wait_ge(sem(f"total_{L}"), 2 * (n + 1))
                    nc.vector.reciprocal(den_inv[:, parity, :], o[:, :, 0]).then_inc(sem(f"normalised_{L}"), 1)
                    dve.wait_ge(sem(f"normalised_{L}"), 2 * n + 1)
                    nc.vector.tensor_tensor(
                        heads_out[:, bass.ds(n * (TB * a.hd), TB * a.hd)].rearrange("p (t d) -> p t d", d=a.hd),
                        o[:, :, 1:a.dv], den_inv[:, parity, :].unsqueeze(2).to_broadcast([P, TB, a.hd]), ALU.mult
                        ).then_inc(sem(f"normalised_{L}"), 1)

                for n in range(AHEAD):
                    for c in range(C):
                        find_max(0, n, c)
                    combine_max(0, n)

                def head(turn, slot):
                    n = RING * turn + slot
                    for k, batch in enumerate(a.batches):
                        if not is_last(turn, slot, AHEAD):
                            for c in batch:
                                find_max(turn + (slot + AHEAD) // RING, (slot + AHEAD) % RING, c)
                        if k == 2 and not is_first(n):
                            normalise(n - 1, (slot + 1) % 2)
                    if not is_last(turn, slot, AHEAD):
                        combine_max(turn + (slot + AHEAD) // RING, (slot + AHEAD) % RING)

                over_heads(dve, head)
                normalise(NH - 1, (NH - 1) % 2)

            def layer_norm(k, chunk_sum):
                for c in range(NCH):
                    chunk_sum(c)
                for t in range(NT):
                    ins = nc.vector.bn_stats(stats[:, t, :], x_plus[:, t, :])
                link(ins)
                for t in range(NT):
                    ins = nc.vector.bn_aggr(mean_var[:, t, :], stats[:, t, :])
                link(ins)
                nc.vector.tensor_scalar(std[:], mean_var[:, :, 1], LN_EPS, None, ALU.add
                                        ).then_inc(sem("var"), 1)
                dve.wait_ge(sem("std"), k)
                link(nc.vector.reciprocal(rstd[:], std[:]))
                for t in range(NT):
                    ins = nc.vector.tensor_scalar(x[:, t, :], x_plus[:, t, :], mean_var[:, t, 0:1], rstd[:, t:t + 1],
                                                  ALU.subtract, ALU.mult)
                    if t % TPC == TPC - 1:
                        ins.then_inc(sem(f"normed_{k}"), 1)

            def after_attention(a):
                L = a.layer

                def chunk_sum(c):
                    t = slice(TPC * c, TPC * (c + 1))
                    dve.wait_ge(sem(f"x_plus_{L}"), c + 1)
                    dve.wait_ge(sem(f"o_ps_{L}"), c + 1)
                    nc.vector.tensor_tensor(x_plus[:, t, :], bank[2 + c % 2][:].rearrange("p (t d) -> p t d", d=D),
                                            x_plus[:, t, :], ALU.add).then_inc(sem(f"summed_{L}"), 1)
                    dve.wait_ge(sem(f"summed_{L}"), c + 1)

                layer_norm(2 * L + 1, chunk_sum)

            def bcast(ap):
                return ap.unsqueeze(2).to_broadcast([P, NT, E])

            def experts(f):
                loaded(dve, f"ffn{f}")
                dve.wait_ge(sem(f"logits_ps_{f}"), 1)
                link(nc.vector.tensor_tensor(logits[:], bank[6][:, 0:NT * E].rearrange("p (t e) -> p t e", e=E),
                                             w_sb[f"br_{f}"][:].unsqueeze(1).to_broadcast([P, NT, E]), ALU.add))
                w1, w2, tmp, inv = (small[:, i, :] for i in (1, 2, 3, 4))
                if f == 1:
                    link(nc.vector.tensor_reduce(tmp, logits[:], AX.X, ALU.max))
                    nc.vector.tensor_tensor(logits[:], logits[:], bcast(tmp), ALU.subtract
                                            ).then_inc(sem(f"route_in_{f}"), 1)
                    dve.wait_ge(sem(f"route_exp_{f}"), 1)
                    link(nc.vector.reduce_sum(tmp, logits[:], AX.X))
                    link(nc.vector.reciprocal(inv, tmp))
                    link(nc.vector.tensor_tensor(logits[:], logits[:], bcast(inv), ALU.mult))
                for t in range(NT):
                    ins = nc.vector.max(top[:, t, :], logits[:, t, :])
                link(ins)
                for t in range(NT):
                    ins = nc.vector.max_index(top_at[:, t, :], top[:, t, :], logits[:, t, :])
                link(ins)
                if f == 0:
                    nc.vector.tensor_tensor(small[:, 0, :], top[:, :, 1], top[:, :, 0], ALU.subtract
                                            ).then_inc(sem(f"route_in_{f}"), 1)
                    dve.wait_ge(sem(f"route_exp_{f}"), 1)
                    link(nc.vector.tensor_scalar(tmp, small[:, 0, :], 1.0, None, ALU.add))
                    link(nc.vector.reciprocal(w1, tmp))
                    link(nc.vector.tensor_tensor(w2, small[:, 0, :], w1, ALU.mult))
                else:
                    link(nc.vector.tensor_tensor(tmp, top[:, :, 0], top[:, :, 1], ALU.add))
                    link(nc.vector.tensor_scalar(tmp, tmp, 1e-8, None, ALU.add))
                    link(nc.vector.reciprocal(inv, tmp))
                    link(nc.vector.tensor_tensor(w1, top[:, :, 0], inv, ALU.mult))
                    link(nc.vector.tensor_tensor(w2, top[:, :, 1], inv, ALU.mult))
                link(nc.vector.tensor_copy(top_f[:], top_at[:, :, 0:2]))
                for i, w in enumerate((w1, w2)):
                    link(nc.vector.tensor_tensor(pick[:, i], iota[:].unsqueeze(1).to_broadcast([P, NT, E]),
                                                 bcast(top_f[:, :, i]), ALU.is_equal))
                    link(nc.vector.tensor_tensor(pick[:, i], pick[:, i], bcast(w), ALU.mult))
                nc.vector.tensor_tensor(gate[:], pick[:, 0], pick[:, 1], ALU.add).then_inc(sem(f"gate_{f}"), 1)
                dve.wait_ge(sem(f"gate_{f}"), 1)
                for c in range(NCH):
                    dve.wait_ge(sem(f"gb_ps_{f}"), c + 1)
                    nc.vector.tensor_copy(acc[:, TPC * c:TPC * (c + 1), :],
                                          bank[4 + c][:].rearrange("p (t d) -> p t d", d=D)
                                          ).then_inc(sem(f"gb_{f}"), 1)
                dve.wait_ge(sem(f"gb_{f}"), NCH)
                for m in range(NCH * E):
                    c, e = m // E, m % E
                    dve.wait_ge(sem(f"y_ps_{f}"), m + 1)
                    ge(dve, f"y_taken_{f}", m)
                    for t in range(TPC):
                        tile = TPC * c + t
                        ins = nc.vector.scalar_tensor_tensor(acc[:, tile, :], bank[4 + m % 2][:, P * t:P * (t + 1)],
                                                             gate[:, tile, e:e + 1], acc[:, tile, :],
                                                             ALU.mult, ALU.add)
                    ins.then_inc(sem(f"y_taken_{f}"), 1)

                def chunk_sum(c):
                    t = slice(TPC * c, TPC * (c + 1))
                    if f == 0:
                        link(nc.vector.tensor_tensor(x_plus[:, t, :], x[:, t, :], acc[:, t, :], ALU.add))
                    else:
                        xt = x[:, t, :].rearrange("p t d -> p (t d)")
                        xp = x_plus[:, t, :].rearrange("p t d -> p (t d)")
                        link(nc.vector.scalar_tensor_tensor(xp, acc[:, t, :].rearrange("p t d -> p (t d)"), MIX, xt,
                                                            ALU.mult, ALU.add))
                        link(nc.vector.tensor_tensor(xp, xp, xt, ALU.add))

                dve.wait_ge(sem(f"y_taken_{f}"), NCH * E)
                layer_norm(2 * f + 2, chunk_sum)

            loaded(dve, "attn0")
            qkv(ATTENTIONS[0])
            attention(ATTENTIONS[0])
            after_attention(ATTENTIONS[0])
            experts(0)
            loaded(dve, "attn1")
            qkv(ATTENTIONS[1])
            attention(ATTENTIONS[1])
            after_attention(ATTENTIONS[1])
            loaded(dve, "attn2")
            qkv(ATTENTIONS[2])
            attention(ATTENTIONS[2])
            experts(1)

        @block.tensor
        def _(pe):
            mm = nc.tensor.matmul

            def transpose_x(k):
                for c in range(NCH):
                    if k == 0:
                        pe.wait_ge(sem("loaded_x"), 16 * NCH)
                    else:
                        pe.wait_ge(sem(f"normed_{k}"), c + 1)
                    if c >= 2:
                        pe.wait_ge(sem(f"xT_{k}"), c - 1)
                    for t in range(TPC):
                        ins = nc.tensor.transpose(bank[c % 2][:, P * t:P * (t + 1)], x[:, TPC * c + t, :], ident[:])
                    ins.then_inc(sem(f"xT_ps_{k}"), 1)

            def effective_weights():
                loaded(pe, "low_rank")
                for w, (a_n, b_n) in enumerate((("q_aT", "q_b"), ("k_aT", "k_b"))):
                    for h in range(H):
                        ins = mm(bank[6 + w][:, 8 * h:8 * h + 8], w_sb[a_n][:, h, :], w_sb[b_n][:, h, :],
                                 start=True, stop=True)
                    ins.then_inc(sem("w_eff_ps"), 1)
                pe.wait_ge(sem("w_eff"), 2)

            def qkv(a, k):
                L = a.layer
                wd = a.width
                wq, wk, wv, *_ = qkv_weights(a)
                items = [(b, w, c) for b in range(B) for w in range(2) for c in range(NCH // B)]
                pe.wait_ge(sem(f"xT_{k}"), NCH)
                for m, (b, w, c) in enumerate(items):
                    if m >= 2:
                        pe.wait_ge(sem(f"part1_{L}"), 2 * (m - 1))
                    mm(bank[2 + m % 2][0:wd, :], (wq, wk)[w], xT[:, S * b + CH * c:S * b + CH * (c + 1)],
                       start=True, stop=True).then_inc(sem(f"qk_ps_{L}"), 1)
                    if m % 2 == 1:
                        cv = m // 2
                        ge(pe, f"v_all_{L}", cv - 1)
                        for t in range(TPC):
                            tile = TPC * cv + t
                            ins = mm(bank[4 + cv % 2][:, P * t:P * t + wd], xT[:, P * tile:P * (tile + 1)], wv,
                                     start=True, stop=True)
                        ins.then_inc(sem(f"v_ps_{L}"), 1)

            def attention(a):
                L = a.layer
                C = a.chunks
                K, KM = a.rows, a.rows_m

                def scores_by_query(turn, slot, c):
                    n = RING * turn + slot
                    s1 = S1[(C * slot + c) % 2]
                    if c == 0:
                        pe.wait_ge(sem(f"qk_in{slot}"), 16 * 2 * PARTS * (turns_before(L) + turn + 1))
                    ge(pe, f"max_taken_{L}", C * n + c - 1)
                    first = True
                    if a.query_diagonal(c):
                        mm(s1[:], ident16[:], mask16[:].rearrange("p t k -> p (t k)"), start=True, stop=False,
                           skip_group_check=True)
                        first = False
                    at = 0
                    for i, k0, count in a.by_query[c]:
                        ins = mm(s1[:, at:at + P * count], qx[0:K, slot, P * i:P * (i + 1)],
                                 kx_of(a)[0:K, slot, P * k0:P * (k0 + count)], start=first, stop=True,
                                 skip_group_check=not first)
                        at += P * count
                    ins.then_inc(sem(f"scores_q_{L}"), 1)

                def scores_by_key(turn, slot, c):
                    n = RING * turn + slot
                    s2 = S2[(C * slot + c) % 2]
                    if c == 0:
                        pe.wait_ge(sem(f"max_in{slot}"), 16 * PARTS * (turns_before(L) + turn + 1))
                    ge(pe, f"probs_{L}", C * n + c - 1)
                    at = 0
                    for j, q0, count, _ in a.by_key[c]:
                        ins = mm(s2[:, at:at + P * count], kx_of(a)[0:KM, slot, P * j:P * (j + 1)],
                                 qx[0:KM, slot, P * q0:P * (q0 + count)], start=True, stop=True)
                        at += P * count
                    ins.then_inc(sem(f"scores_k_{L}"), 1)

                def max_rows(turn, slot):
                    n = RING * turn + slot
                    pe.wait_ge(sem(f"neg_parts_{L}"), 4 * (n + 1))
                    ge(pe, f"by_quarter_{L}", 2 * (n - 2))
                    nc.tensor.transpose(neg_ps, neg_parts[:, slot].rearrange("p c t -> p (c t)"), ident16[:]
                                        ).then_inc(sem(f"neg_ps_{L}"), 1)

                order = [(c, b, q0 // 4, quarter) for c in range(C) for b, (_, q0, _, quarter) in enumerate(a.by_key[c])]
                opens = {next(m for m in order if m[2:] == hq) for hq in {m[2:] for m in order}}
                closes = {next(m for m in reversed(order) if m[2:] == hq) for hq in {m[2:] for m in order}}

                def probs_by_v(turn, slot, c):
                    n = RING * turn + slot
                    if c == 0:
                        pe.wait_ge(sem(f"v_head_{L}"), n + 1)
                        ge(pe, f"sums_{L}", 2 * n)
                    if c in a.masked:
                        pe.wait_ge(sem(f"masked_{L}"), 2 * n + a.masked.index(c) + 1)
                    else:
                        pe.wait_ge(sem(f"probs_{L}"), C * n + c + 1)
                    at = 0
                    for b, (j, q0, count, quarter) in enumerate(a.by_key[c]):
                        half, q = q0 // 4, P * (q0 % 4)
                        this = (c, b, half, quarter)
                        ins = mm(SUM[half][Q * quarter:Q * (quarter + 1), q:q + P * count], v_head[:, slot, j, :],
                                 probs[:, (C * slot + c) % a.probs_ring, at:at + P * count],
                                 start=this in opens, stop=this in closes, skip_group_check=True)
                        at += P * count
                    ins.then_inc(sem(f"pv_{L}"), 1)

                def turn_sums(n, parity):
                    pe.wait_ge(sem(f"sums_{L}"), 2 * (n + 1))
                    ge(pe, f"by_quarter_{L}", 2 * n)
                    if not (isinstance(n, int) and n == NH - 1):
                        pe.wait_ge(sem(f"neg_rows_{L}"), min(n + 3, NH) if isinstance(n, int) else n + 3)
                    for i in range(TB):
                        ins = nc.tensor.transpose(OUT[i // 4][:, P * (i % 4):P * (i % 4 + 1)],
                                                  sums[:, parity, i // 4, P * (i % 4):P * (i % 4 + 1)], ident[:])
                    ins.then_inc(sem(f"out_{L}"), 1)

                for n in range(AHEAD):
                    for c in range(C):
                        scores_by_query(0, n, c)
                max_rows(0, 0)

                def head(turn, slot):
                    n = RING * turn + slot
                    for k, batch in enumerate(a.batches):
                        for c in batch:
                            if not is_last(turn, slot, AHEAD):
                                scores_by_query(turn + (slot + AHEAD) // RING, (slot + AHEAD) % RING, c)
                            scores_by_key(turn, slot, c)
                        if k == 0 and not is_last(turn, slot, 1):
                            max_rows(turn + (slot + 1) // RING, (slot + 1) % RING)
                        if k == 1 and not is_first(n):
                            turn_sums(n - 1, (slot + 1) % 2)
                        if k > 0:
                            for c in a.batches[k - 1]:
                                probs_by_v(turn, slot, c)
                        elif not is_first(n):
                            for c in a.batches[-1]:
                                probs_by_v(turn + (slot + 3) // RING - 1, (slot + 3) % RING, c)

                over_heads(pe, head)
                for c in a.batches[-1]:
                    probs_by_v(NH // RING - 1, RING - 1, c)
                turn_sums(NH - 1, (NH - 1) % 2)

            def transpose_a(a, c):
                for t in range(TPC):
                    pe.wait_ge(sem(f"a_tok_{a.layer}"), TPC * c + t + 1)
                    if t == 0:
                        ge(pe, f"aT_{a.layer}", c - 1)
                    ins = nc.tensor.transpose(bank[c % 2][0:a.width, P * t:P * (t + 1)],
                                              a_tok[:, TPC * c + t, 0:a.width], ident[:])
                ins.then_inc(sem(f"aT_ps_{a.layer}"), 1)

            def project(a):
                L = a.layer
                transpose_a(a, 0)
                for c in range(NCH):
                    if c + 1 < NCH:
                        transpose_a(a, c + 1)
                    pe.wait_ge(sem(f"aT_{L}"), c + 1)
                    if c >= 2:
                        pe.wait_ge(sem(f"summed_{L}"), c - 1)
                    for t in range(TPC):
                        tile = TPC * c + t
                        ins = mm(bank[2 + c % 2][:, P * t:P * (t + 1)], aT[:, P * tile:P * (tile + 1)],
                                 w_sb[f"woT{L}"][:], start=True, stop=True)
                    ins.then_inc(sem(f"o_ps_{L}"), 1)

            def project_mla(a):
                transpose_a(a, 0)
                for c in range(NCH):
                    if c + 1 < NCH:
                        transpose_a(a, c + 1)
                    pe.wait_ge(sem(f"aT_{a.layer}"), c + 1)
                    ge(pe, "mla", c - 1)
                    mm(bank[2 + c % 2][:], w_sb["wo2"][:], aT[0:a.width, CH * c:CH * (c + 1)], start=True, stop=True
                       ).then_inc(sem("mla_ps"), 1)

            def experts(f):
                loaded(pe, f"ffn{f}")
                pe.wait_ge(sem("xT_1" if f == 0 else "mla"), NCH)
                for t in range(NT):
                    ins = mm(bank[6][:, E * t:E * (t + 1)], xT[:, P * t:P * (t + 1)], w_sb[f"wr_{f}"][:],
                             start=True, stop=True)
                ins.then_inc(sem(f"logits_ps_{f}"), 1)

                def up(m):
                    c, e = m // E, m % E
                    ge(pe, f"hid_{f}", 2 * (m - 1))
                    for fb in range(FB):
                        ins = mm(bank[2 * (m % 2) + fb][:], w_sb[f"w1_{f}"][:, e, P * fb:P * (fb + 1)],
                                 xT[:, CH * c:CH * (c + 1)], start=True, stop=True)
                    ins.then_inc(sem(f"hid_ps_{f}"), 1)

                def down(m):
                    e = m % E
                    if m < 2:
                        pe.wait_ge(sem(f"gb_{f}"), NCH)
                    ge(pe, f"y_taken_{f}", m - 1)
                    pe.wait_ge(sem(f"hid_{f}"), 2 * (m + 1))
                    for t in range(TPC):
                        for fb in range(FB):
                            ins = mm(bank[4 + m % 2][:, P * t:P * (t + 1)], hidden[:, m % 2, fb, P * t:P * (t + 1)],
                                     w_sb[f"w2_{f}"][:, e, fb, :], start=fb == 0, stop=fb == FB - 1)
                    ins.then_inc(sem(f"y_ps_{f}"), 1)

                pe.wait_ge(sem(f"gate_{f}"), 1)
                for c in range(NCH):
                    for t in range(TPC):
                        ins = nc.tensor.transpose(bank[4 + c][0:E, P * t:P * (t + 1)], gate[:, TPC * c + t, :], ident[:])
                    ins.then_inc(sem(f"gateT_ps_{f}"), 1)
                for c in range(NCH):
                    pe.wait_ge(sem(f"gateT_{f}"), c + 1)
                    for t in range(TPC):
                        tile = TPC * c + t
                        ins = mm(bank[4 + c][:, P * t:P * (t + 1)], gateT[:, P * tile:P * (tile + 1)],
                                 w_sb[f"b2_{f}"][:], start=True, stop=True)
                    ins.then_inc(sem(f"gb_ps_{f}"), 1)
                up(0)
                for m in range(NCH * E):
                    if m + 1 < NCH * E:
                        up(m + 1)
                    down(m)

            pe.wait_ge(sem("constants"), CONSTANTS)
            effective_weights()
            loaded(pe, "attn0")
            transpose_x(0)
            qkv(ATTENTIONS[0], 0)
            attention(ATTENTIONS[0])
            project(ATTENTIONS[0])
            transpose_x(1)
            experts(0)
            transpose_x(2)
            loaded(pe, "attn1")
            qkv(ATTENTIONS[1], 2)
            attention(ATTENTIONS[1])
            project(ATTENTIONS[1])
            transpose_x(3)
            loaded(pe, "attn2")
            qkv(ATTENTIONS[2], 3)
            attention(ATTENTIONS[2])
            project_mla(ATTENTIONS[2])
            experts(1)


CONSTANTS = 15


def kernel(**inputs):
    import numpy as np
    import concourse.bacc as bacc
    from concourse import mybir as _mybir
    from concourse.bass_utils import run_bass_kernel_spmd

    g = {n: np.asarray(v) for n, v in inputs.items()}
    f32 = np.float32
    nc = bacc.Bacc("TRN2", target_bir_lowering=False, num_devices=1)
    arrays, inp = {}, {}

    def give(name, a, group):
        a = np.ascontiguousarray(a)
        arrays["in_" + name] = a
        inp[name] = (nc.dram_tensor("in_" + name, a.shape, _mybir.dt.from_np(a.dtype), kind="ExternalInput").ap(), group)

    def over_tokens(row):
        return np.broadcast_to(row.reshape(1, -1), (P, row.size))

    give("x", g["L0_attn_x"].reshape(T, D), "x")
    give("q_aT", g["L1_attn_q_a"].transpose(2, 0, 1), "low_rank")
    give("q_b", g["L1_attn_q_b"].transpose(1, 0, 2), "low_rank")
    give("k_aT", g["L1_attn_k_a"].transpose(2, 0, 1), "low_rank")
    give("k_b", g["L1_attn_k_b"].transpose(1, 0, 2), "low_rank")
    give("wqT0", g["L0_attn_Wq"].T, "attn0")
    give("wkT0", g["L0_attn_Wk"].T, "attn0")
    give("wvT0", g["L0_attn_Wv"].T, "attn0")
    give("woT0", g["L0_attn_Wo"].T, "attn0")
    give("bq0", g["L0_attn_bq"].reshape(D, 1), "attn0")
    give("bk0", g["L0_attn_bk"].reshape(D, 1), "attn0")
    give("bv0", over_tokens(g["L0_attn_bv"]), "attn0")
    give("bo0", over_tokens(g["L0_attn_bo"]), "attn0")

    def experts(f, wr, br, w1, b1, w2, b2):
        give(f"wr_{f}", g[wr], f"ffn{f}")
        give(f"br_{f}", over_tokens(g[br]), f"ffn{f}")
        give(f"w1_{f}", g[w1].transpose(1, 0, 2), f"ffn{f}")
        give(f"b1_{f}", g[b1].reshape(E * FB, P).T, f"ffn{f}")
        give(f"w2_{f}", g[w2].reshape(E, FB, P, D).transpose(2, 0, 1, 3), f"ffn{f}")
        give(f"b2_{f}", g[b2], f"ffn{f}")

    experts(0, "L0_ffn_Wr", "L0_ffn_br", "L0_ffn_W1", "L0_ffn_b1", "L0_ffn_W2", "L0_ffn_b2")
    give("wvT1", g["L1_attn_v_w"].T, "attn1")
    give("woT1", g["L1_attn_o_w"].T, "attn1")
    give("bv1", over_tokens(g["L1_attn_v_b"]), "attn1")
    give("bo1", over_tokens(g["L1_attn_o_b"]), "attn1")
    lat = D // 2
    kph = lat // H
    give("wq2", g["L1_ffn_q_w"].reshape(D, H, D // H)[:, :, :kph].reshape(D, lat), "attn2")
    give("wk2", g["L1_ffn_k_w"], "attn2")
    give("wv2", g["L1_ffn_v_w"], "attn2")
    give("wo2", g["L1_ffn_o_w"][:lat], "attn2")
    give("bq2", g["L1_ffn_q_b"].reshape(H, D // H)[:, :kph].reshape(lat, 1), "attn2")
    give("bk2", g["L1_ffn_k_b"].reshape(lat, 1), "attn2")
    give("bv2", over_tokens(g["L1_ffn_v_b"]), "attn2")
    give("bo2", g["L1_ffn_o_b"].reshape(D, 1), "attn2")
    experts(1, "L1_ffn_router_w", "L1_ffn_router_b", "L1_ffn_w1", "L1_ffn_b1", "L1_ffn_w2", "L1_ffn_b2")

    out = nc.dram_tensor("out_x", (T, D), F32, kind="ExternalOutput").ap()
    build(nc, inp, out)
    r = run_bass_kernel_spmd(nc, [arrays], core_ids=[0])
    return r.results[0]["out_x"].reshape(B, S, D)
```

```python
from contextlib import ExitStack

import concourse.bass as bass
from concourse import mybir

ALU = mybir.AluOpType
ACT = mybir.ActivationFunctionType
AX = mybir.AxisListType
F32 = mybir.dt.float32
BF16 = mybir.dt.bfloat16
U32 = mybir.dt.uint32
I32 = mybir.dt.int32

P = 128
B, S, D = 2, 1024, 128
T = B * S
NT = T // P
TB = S // P
H = 16
NH = B * H
E = 8
F = 2 * D
FB = F // P
CH = 512
NCH = T // CH
TPC = CH // P
BY_SEQUENCE = ((0, 1), (2, 3))
LAST_APART = ((0, 1, 2), (3,))
PARTS = 3
RING = 4
AHEAD = 2
Q = 32
LOWEST = -3.0e38
LN_EPS = 1e-5
RANK = 64
MIX = 0.3


class Attention:

    def __init__(self, layer, head_dim, scale_dim, causal):
        self.layer = layer
        self.hd = head_dim
        self.width = H * head_dim
        self.rows = PARTS * PARTS * head_dim
        self.rows_m = self.rows + PARTS
        self.dv = head_dim + 1
        self.scale = float(scale_dim) ** -0.5
        self.causal = causal
        if causal:
            diagonal = [[(i, i, 1) for i in range(4 * c, 4 * c + 4)] for c in range(2)]
            self.by_query = diagonal + [
                [(7, 0, 4)], [(7, 4, 3), (1, 0, 1)], [(6, 0, 4)], [(6, 4, 2), (2, 0, 2)],
                [(5, 0, 4)], [(5, 4, 1), (3, 0, 3)], [(4, 0, 4)]]
            self.maxima = 3
            self.by_key = [
                [(i, i, 1, 3) for i in range(4)], [(0, 4, 4, 0)], [(1, 4, 4, 1)],
                [(0, 1, 3, 3), (2, 3, 1, 3)], [(2, 4, 4, 2)], [(3, 4, 4, 0)],
                [(4, 4, 1, 1), (5, 5, 1, 2), (6, 6, 1, 1), (7, 7, 1, 2)], [(1, 2, 2, 3), (5, 6, 2, 0)],
                [(4, 5, 3, 1), (6, 7, 1, 2)]]
            self.masked = (0, 6)
            self.batch = 3
            self.adds = 3
        else:
            self.by_query = [[(i, 4 * c, 4)] for i in range(TB) for c in range(2)]
            self.maxima = 2
            self.by_key = [[(j, 4 * half, 4, 2 * half + j % 2)] for two in range(0, TB, 2) for half in range(2)
                           for j in range(two, two + 2)]
            self.masked = ()
            self.batch = 4
            self.adds = 1
        self.chunks = len(self.by_key)
        self.bank_of = [c % 3 for c in range(self.chunks)]
        if self.chunks % 3 == 1:
            self.bank_of[-1] = 1
        self.bank_back = [next(d for d in range(1, 9) if self.bank_of[c - d] == self.bank_of[c])
                          for c in range(self.chunks)]
        self.batches = [range(c, c + self.batch) for c in range(0, self.chunks, self.batch)]
        self.probs_ring = 2 * self.batch

    def query_diagonal(self, c):
        return self.causal and c < 2


ATTENTIONS = [Attention(0, 8, 8, True), Attention(1, 8, 8, True), Attention(2, 4, 4, False)]


def build(nc, inp, out):
    ctx = ExitStack()
    with ctx:
        def sb(name, shape, dt=F32):
            return ctx.enter_context(nc.sbuf_tensor(name, shape, dt))

        sems = {}

        def sem(name):
            if name not in sems:
                sems[name] = ctx.enter_context(nc.semaphore(name))
            return sems[name]

        qk_dram = [[nc.dram_tensor(f"{w}_parts_{a.layer}", (PARTS, B, a.width, S), BF16, kind="Internal").ap()
                    for w in "qk"] for a in ATTENTIONS]

        x = sb("x", [P, NT, D])
        xT = sb("xT", [P, T])
        x_plus = sb("x_plus", [P, NT, D])
        acc = sb("acc", [P, NT, D])
        parts = [sb("q_parts", [P, PARTS, T], BF16), sb("k_parts", [P, PARTS, T], BF16)]
        whole = sb("whole", [P, 2, CH])
        rest = sb("rest", [P, 2, CH])
        qx = sb("qx", [P, RING, S], BF16)
        kx = sb("kx", [P, RING, S], BF16)
        kx4 = sb("kx4", [P, RING, S], BF16)
        v_all = [sb("v8", [P, NH, TB, 9]), sb("v4", [P, NH, TB, 5])]
        v_head = sb("v_head", [P, RING, TB, Q])
        probs = sb("probs", [P, 8, CH])
        sums = sb("sums", [P, 2, CH])
        by_quarter = sb("by_quarter", [P, 2, 4, 4, 9])
        pairs = sb("pairs", [P, 4, 9])
        total = sb("total", [P, 2, TB, 9])
        tile_max = sb("tile_max", [P, RING, TB, 3])
        neg_max = sb("neg_max", [P, RING, TB])
        neg_rest = sb("neg_rest", [P, 2, TB])
        neg_parts = sb("neg_parts", [P, RING, PARTS, TB], BF16)
        neg_rows = sb("neg_rows", [PARTS * TB, RING, P], BF16)
        den_inv = sb("den_inv", [P, 2, TB])
        heads_out = sb("heads_out", [P, NH * TB * 8])
        a_tok = sb("a_tok", [P, NT, D])
        aT = sb("aT", [P, T])
        hidden = probs[:, 0:4, :].rearrange("p (m f) c -> p m f c", f=FB)
        stats = sb("stats", [P, NT, 6])
        mean_var = sb("mean_var", [P, NT, 2])
        std = sb("std", [P, NT])
        rstd = sb("rstd", [P, NT])
        logits = sb("logits", [P, NT, E])
        top = sb("top", [P, NT, E])
        top_at = sb("top_at", [P, NT, E], U32)
        top_f = sb("top_f", [P, NT, 2])
        small = sb("small", [P, 6, NT])
        pick = sb("pick", [P, 2, NT, E])
        gate = sb("gate", [P, NT, E])
        gateT = aT[0:E, :]
        iota_i = sb("iota_i", [P, E], I32)
        iota = sb("iota", [P, E])
        ident = sb("ident", [P, P])
        ident16 = sb("ident16", [P, P], BF16)
        mask16 = sb("mask16", [P, 4, P], BF16)
        w_sb = {n: sb("sb_" + n, list(ap.shape)) for n, (ap, _) in inp.items()
                if n not in ("x", "q_aT", "k_aT")}
        w_sb["q_aT"] = acc[0:RANK]
        w_sb["k_aT"] = a_tok[0:RANK]
        w_eff = [sb("wq_eff", [P, D]), sb("wk_eff", [P, D])]

        bank = [ctx.enter_context(nc.psum_tensor(f"bank{i}", [P, CH], F32)) for i in range(8)]
        S1 = [bank[0], bank[1], bank[6]]
        S2 = [bank[2], bank[3], bank[5]]
        SUM = bank[4]
        OUT = bank[7]
        neg_ps = bank[7][0:PARTS * TB, 0:P // 2].bitcast(BF16)

        def kx_of(a):
            return kx if a.hd == 8 else kx4

        def v_of(a):
            return v_all[0 if a.hd == 8 else 1]

        groups = {}
        for n, (ap, g) in inp.items():
            if n != "x":
                groups.setdefault(g, []).append(n)

        def loaded(eng, g):
            eng.wait_ge(sem(f"loaded_{g}"), 16 * len(groups[g]))

        def ge(eng, name, value):
            if isinstance(value, int) and value <= 0:
                return
            eng.wait_ge(sem(name), value)

        def qkv_weights(a):
            if a.layer == 0:
                return w_sb["wqT0"][:], w_sb["wkT0"][:], w_sb["wvT0"][:], w_sb["bv0"], w_sb["bq0"], w_sb["bk0"]
            if a.layer == 1:
                return w_eff[0][:], w_eff[1][:], w_sb["wvT1"][:], w_sb["bv1"], None, None
            return w_sb["wq2"][:], w_sb["wk2"][:], w_sb["wv2"][:], w_sb["bv2"], w_sb["bq2"], w_sb["bk2"]

        block = ctx.enter_context(nc.Block())

        def over_heads(eng, head):
            for slot in range(RING):
                head(0, slot)
            with eng.Fori(1, NH // RING - 1) as turn:
                for slot in range(RING):
                    head(turn, slot)
            for slot in range(RING):
                head(NH // RING - 1, slot)

        def turns_before(layer):
            return layer * (NH // RING)

        def is_first(n):
            return isinstance(n, int) and n == 0

        def is_last(turn, slot, ahead):
            return isinstance(turn, int) and RING * turn + slot + ahead >= NH

        @block.sync
        def _(sp):
            for c in range(NCH):
                sp.dma_start(x[:, TPC * c:TPC * (c + 1), :],
                             inp["x"][0].rearrange("(t p) d -> p t d", p=P)[:, TPC * c:TPC * (c + 1), :]
                             ).then_inc(sem("loaded_x"), 16)
            for g in groups:
                for n in groups[g]:
                    sp.dma_start(w_sb[n][:], inp[n][0]).then_inc(sem(f"loaded_{g}"), 16)

            def attention(a):
                L = a.layer
                C = a.chunks

                def store_parts(b):
                    for w in range(2):
                        sp.wait_ge(sem(f"part3_{L}"), (2 * b + w + 1) * (NCH // B))
                        for p in range(PARTS):
                            sp.dma_start(qk_dram[L][w][p, b], parts[w][0:a.width, p, S * b:S * (b + 1)]
                                         ).then_inc(sem(f"parts_out{b}_{L}"), 16)
                    sp.wait_ge(sem(f"parts_out{b}_{L}"), 16 * 2 * PARTS)

                def by_head(w):
                    return qk_dram[L][w].rearrange("c b (h d) t -> c (b h) d t", d=a.hd)

                def load_head(turn, slot):
                    n = RING * turn + slot
                    rows = PARTS * a.hd
                    for i in range(PARTS):
                        q = by_head(0)[i:i + 1, bass.ds(n, 1)].rearrange("c n d t -> (c n) d t").to_broadcast([PARTS, a.hd, S])
                        sp.dma_start(qx[rows * i:rows * (i + 1), slot, :], q).then_inc(sem(f"qk_in{slot}"), 16)
                        k = by_head(1)[:, bass.ds(n, 1)].rearrange("c n d t -> (c n) d t")
                        sp.dma_start(kx_of(a)[rows * i:rows * (i + 1), slot, :], k).then_inc(sem(f"qk_in{slot}"), 16)

                def load_max(turn, slot):
                    for p in range(PARTS):
                        sp.dma_start(qx[a.rows + p:a.rows + p + 1, slot, :],
                                     neg_rows[TB * p:TB * (p + 1), slot, :]).then_inc(sem(f"max_in{slot}"), 16)

                if L == 0:
                    sp.wait_ge(sem("constants"), CONSTANTS)
                store_parts(0)
                for n in range(AHEAD + 1):
                    load_head(0, n)
                store_parts(1)
                ge(sp, f"neg_rows_{L}", 1)
                load_max(0, 0)

                def head(turn, slot):
                    n = RING * turn + slot
                    if not is_last(turn, slot, 3):
                        ge(sp, f"scores_k_{L}", C * n)
                        load_head(turn + (slot + 3) // RING, (slot + 3) % RING)
                    if not is_last(turn, slot, 1):
                        ge(sp, f"neg_rows_{L}", n + 2)
                        load_max(turn + (slot + 1) // RING, (slot + 1) % RING)

                over_heads(sp, head)

            for a in ATTENTIONS:
                attention(a)
            for c in range(NCH):
                sp.wait_ge(sem("normed_4"), c + 1)
                sp.dma_start(out.rearrange("(t p) d -> p t d", p=P)[:, TPC * c:TPC * (c + 1), :],
                             x[:, TPC * c:TPC * (c + 1), :]).then_inc(sem("stored"), 16)
            sp.wait_ge(sem("stored"), 16 * NCH)

        @block.gpsimd
        def _(pool):
            made = [0]

            def constant(ins):
                made[0] += 1
                ins.then_inc(sem("constants"), 1)

            constant(nc.gpsimd.memset(ident[:], 0.0))
            constant(nc.gpsimd.memset(ident16[:], 0.0))
            constant(nc.gpsimd.memset(mask16[:], 0.0))
            pool.wait_ge(sem("constants"), made[0])
            for m in (ident, ident16):
                constant(nc.gpsimd.affine_select(out=m[:], in_=m[:], compare_op=ALU.not_equal, fill=1.0, base=0,
                                                 pattern=[[-1, P]], channel_multiplier=1))
            constant(nc.gpsimd.affine_select(out=mask16[:], in_=mask16[:], compare_op=ALU.is_ge, fill=LOWEST, base=0,
                                             pattern=[[0, 4], [-1, P]], channel_multiplier=1))
            constant(nc.gpsimd.memset(tile_max[:], LOWEST))
            constant(nc.gpsimd.memset(kx[:], 1.0))
            constant(nc.gpsimd.memset(kx4[:], 1.0))
            for v in v_all:
                constant(nc.gpsimd.memset(v[:, :, :, 0:1], 1.0))
            constant(nc.gpsimd.memset(v_head[:], 0.0))
            constant(nc.gpsimd.iota(iota_i[:], pattern=[[1, E]], base=0, channel_multiplier=0))
            pool.wait_ge(sem("constants"), made[0])
            constant(nc.gpsimd.tensor_copy(iota[:], iota_i[:]))
            assert made[0] == CONSTANTS

            def add_bias(L):
                loaded(pool, f"attn{L}")
                if L == 0:
                    pool.wait_ge(sem("loaded_x"), 16 * NCH)
                else:
                    pool.wait_ge(sem(f"normed_{2 * L}"), NCH)
                for c in range(NCH):
                    t = slice(TPC * c, TPC * (c + 1))
                    nc.gpsimd.tensor_tensor(x_plus[:, t, :], x[:, t, :],
                                            w_sb[f"bo{L}"][:].unsqueeze(1).to_broadcast([P, TPC, D]), ALU.add
                                            ).then_inc(sem(f"x_plus_{L}"), 1)

            def gather_heads(a, tiles):
                src = heads_out[:, 0:NH * TB * a.hd].rearrange("p (b h t d) -> p b h t d", b=B, h=H, t=TB)
                for t in tiles:
                    nc.gpsimd.tensor_copy(a_tok[:, t, 0:a.width].rearrange("p (h d) -> p h d", h=H),
                                          src[:, t // TB, :, t % TB, :]).then_inc(sem(f"a_tok_{a.layer}"), 1)

            def attention(a):
                L = a.layer
                C = a.chunks

                def apart(name, value):
                    if not isinstance(value, int):
                        value = pool.to_reg(value)
                        pool.wait_ge(sem("constants"), CONSTANTS)
                    ge(pool, name, value)

                def take_v(turn, slot):
                    n = RING * turn + slot
                    ge(pool, f"pv_{L}", C * (n - 3))
                    nc.gpsimd.tensor_copy(v_head[:, slot, :, 0:a.dv],
                                          v_of(a)[:, bass.ds(n, 1), :, :].rearrange("p n t d -> p (n t) d")
                                          ).then_inc(sem(f"v_head_{L}"), 1)

                def split_max(turn, slot):
                    n = RING * turn + slot
                    whole_m, rest_m = neg_max[:, slot, :], neg_rest[:, slot % 2, :]
                    ge(pool, f"neg_ps_{L}", n - 3)
                    apart(f"neg_max_{L}", n + 1)
                    nc.gpsimd.tensor_copy(neg_parts[:, slot, 0, :], whole_m).then_inc(sem(f"neg_parts_{L}"), 1)
                    pool.wait_ge(sem(f"neg_parts_{L}"), 4 * n + 1)
                    nc.gpsimd.tensor_tensor(rest_m, whole_m, neg_parts[:, slot, 0, :], ALU.subtract
                                            ).then_inc(sem(f"neg_parts_{L}"), 1)
                    apart(f"neg_parts_{L}", 4 * n + 2)
                    nc.gpsimd.tensor_copy(neg_parts[:, slot, 1, :], rest_m).then_inc(sem(f"neg_parts_{L}"), 1)
                    pool.wait_ge(sem(f"neg_parts_{L}"), 4 * n + 3)
                    nc.gpsimd.tensor_tensor(neg_parts[:, slot, 2, :], rest_m, neg_parts[:, slot, 1, :], ALU.subtract
                                            ).then_inc(sem(f"neg_parts_{L}"), 1)

                pool.wait_ge(sem(f"v_all_{L}"), NCH)
                for n in range(AHEAD):
                    take_v(0, n)
                for n in range(AHEAD):
                    split_max(0, n)

                def add_quarters(n, parity):
                    q = by_quarter[:, parity, :, :, 0:a.dv]
                    pool.wait_ge(sem(f"by_quarter_{L}"), n + 1)
                    if not a.causal:
                        ge(pool, f"normalised_{L}", 2 * (n - 1))
                        nc.gpsimd.tensor_tensor(
                            total[:, parity, :, 0:a.dv].rearrange("p (half t) d -> p t half d", half=2),
                            q[:, :, 0:4:2, :], q[:, :, 1:4:2, :], ALU.add).then_inc(sem(f"total_{L}"), 1)
                        return
                    ge(pool, f"total_{L}", a.adds * n)
                    nc.gpsimd.tensor_tensor(pairs[:], q[:, :, 0, :], q[:, :, 1, :], ALU.add
                                            ).then_inc(sem(f"total_{L}"), 1)
                    pool.wait_ge(sem(f"total_{L}"), a.adds * n + 1)
                    ge(pool, f"normalised_{L}", 2 * (n - 1))
                    nc.gpsimd.tensor_tensor(total[:, parity, 4:8, :], pairs[:], q[:, :, 2, :], ALU.add
                                            ).then_inc(sem(f"total_{L}"), 1)
                    nc.gpsimd.tensor_copy(total[:, parity, 0:4, :], q[:, :, 3, :]).then_inc(sem(f"total_{L}"), 1)

                def mask(turn, slot, which):
                    n = RING * turn + slot
                    c = a.masked[which]
                    p = probs[:, (C * slot + c) % a.probs_ring, :].rearrange("p (t q) -> p t q", q=P)
                    apart(f"probs_{L}", C * n + c + 1)
                    nc.gpsimd.affine_select(out=p, in_=p, compare_op=ALU.is_ge, fill=0.0, base=0,
                                            pattern=[[0, 4], [1, P]], channel_multiplier=-1
                                            ).then_inc(sem(f"masked_{L}"), 1)

                def head(turn, slot):
                    ahead = (turn + (slot + AHEAD) // RING, (slot + AHEAD) % RING)
                    if a.causal:
                        mask(turn, slot, 0)
                    if not is_last(turn, slot, AHEAD):
                        take_v(*ahead)
                    if not is_first(RING * turn + slot):
                        add_quarters(RING * turn + slot - 1, (slot + 1) % 2)
                    if a.causal:
                        mask(turn, slot, 1)
                    if not is_last(turn, slot, AHEAD):
                        split_max(*ahead)
                    if isinstance(turn, int) and turn > 0:
                        pool.wait_ge(sem(f"normalised_{L}"), NH)
                        gather_heads(a, range(slot * TB // RING, (slot + 1) * TB // RING))

                over_heads(pool, head)
                add_quarters(NH - 1, (NH - 1) % 2)
                pool.wait_ge(sem(f"normalised_{L}"), 2 * NH)
                gather_heads(a, range(TB, NT))

            def third_parts(a):
                L = a.layer
                items = [(b, w, c) for b in range(B) for w in range(2) for c in range(NCH // B)]
                for m, (b, w, c) in enumerate(items):
                    t = slice(S * b + CH * c, S * b + CH * (c + 1))
                    pool.wait_ge(sem(f"part2_{L}"), m + 1)
                    nc.gpsimd.tensor_tensor(parts[w][0:a.width, 2, t], rest[0:a.width, m % 2, :],
                                            parts[w][0:a.width, 1, t], ALU.subtract).then_inc(sem(f"part3_{L}"), 1)

            for a in ATTENTIONS:
                third_parts(a)
                if a.layer < 2:
                    add_bias(a.layer)
                attention(a)

        @block.scalar
        def _(act):
            def transposed(k, chunks):
                for c in chunks:
                    act.wait_ge(sem(f"xT_ps_{k}"), c + 1)
                    nc.scalar.activation(xT[:, CH * c:CH * (c + 1)], bank[c % 2][:], ACT.Copy
                                         ).then_inc(sem(f"xT_{k}"), 1)

            def effective_weights():
                for w in range(2):
                    act.wait_ge(sem("w_eff_ps"), w + 1)
                    nc.scalar.activation(w_eff[w][:], bank[6 + w][:, 0:D], ACT.Copy).then_inc(sem("w_eff"), 1)

            def qkv(a, k):
                L = a.layer
                wd = a.width
                *_, bq, bk = qkv_weights(a)
                items = [(b, w, c) for b in range(B) for w in range(2) for c in range(NCH // B)]

                def second(m):
                    b, w, c = items[m]
                    t = slice(S * b + CH * c, S * b + CH * (c + 1))
                    act.wait_ge(sem(f"rest_{L}"), m + 1)
                    nc.scalar.activation(parts[w][0:wd, 1, t], rest[0:wd, m % 2, :], ACT.Copy
                                         ).then_inc(sem(f"part2_{L}"), 1)

                for m, (b, w, c) in enumerate(items):
                    if m == len(items) // B:
                        transposed(k, BY_SEQUENCE[1])
                    t = slice(S * b + CH * c, S * b + CH * (c + 1))
                    act.wait_ge(sem(f"qk_ps_{L}"), m + 1)
                    if m >= 2:
                        act.wait_ge(sem(f"rest_{L}"), m - 1)
                    bias = (bq, bk)[w]
                    kw = {} if bias is None else {"bias": bias[0:wd, :]}
                    nc.scalar.activation(whole[0:wd, m % 2, :], bank[2 + m % 2][0:wd, :], ACT.Identity, **kw
                                         ).then_inc(sem(f"part1_{L}"), 1)
                    nc.scalar.activation(parts[w][0:wd, 0, t], bank[2 + m % 2][0:wd, :], ACT.Identity, **kw
                                         ).then_inc(sem(f"part1_{L}"), 1)
                    if m >= 1:
                        second(m - 1)
                second(len(items) - 1)

            def attention(a):
                L = a.layer
                C = a.chunks

                def rows(turn, slot):
                    n = RING * turn + slot
                    act.wait_ge(sem(f"neg_ps_{L}"), n + 1)
                    ge(act, f"max_in{slot}", 16 * PARTS * (turns_before(L) + turn))
                    nc.scalar.activation(neg_rows[:, slot, :], neg_ps, ACT.Copy
                                         ).then_inc(sem(f"neg_rows_{L}"), 1)

                def take_sums(n, parity):
                    act.wait_ge(sem(f"pv_{L}"), C * (n + 1))
                    ge(act, f"out_{L}", n - 1)
                    nc.scalar.activation(sums[:, parity, :], SUM[:], ACT.Copy).then_inc(sem(f"sums_{L}"), 1)

                def take_out(n, parity):
                    act.wait_ge(sem(f"out_{L}"), n + 1)
                    ge(act, f"total_{L}", a.adds * (n - 1))
                    nc.scalar.activation(by_quarter[:, parity, :, :, 0:a.dv],
                                         OUT[:].rearrange("p (t g c) -> p t g c", t=4, g=4)[:, :, :, 0:a.dv],
                                         ACT.Copy).then_inc(sem(f"by_quarter_{L}"), 1)

                rows(0, 0)

                def head(turn, slot):
                    n = RING * turn + slot
                    for k, batch in enumerate(a.batches):
                        for c in batch:
                            act.wait_ge(sem(f"scores_k_{L}"), C * n + c + 1)
                            ge(act, f"pv_{L}", C * n + c - a.probs_ring + 1)
                            nc.scalar.activation(probs[:, (C * slot + c) % a.probs_ring, :],
                                                 S2[a.bank_of[c]][:], ACT.Exp, scale=a.scale
                                                 ).then_inc(sem(f"probs_{L}"), 1)
                        if k == 0 and not is_last(turn, slot, 1):
                            rows(turn + (slot + 1) // RING, (slot + 1) % RING)
                        if k == 0 and not is_first(n):
                            take_sums(n - 1, (slot + 1) % 2)
                        if k == 1 and not is_first(n):
                            take_out(n - 1, (slot + 1) % 2)

                over_heads(act, head)
                take_sums(NH - 1, (NH - 1) % 2)
                take_out(NH - 1, (NH - 1) % 2)

            def projected(a):
                for c in range(NCH):
                    act.wait_ge(sem(f"aT_ps_{a.layer}"), c + 1)
                    nc.scalar.activation(aT[0:a.width, CH * c:CH * (c + 1)], bank[c % 2][0:a.width, :], ACT.Copy
                                         ).then_inc(sem(f"aT_{a.layer}"), 1)

            def mla():
                for c in range(NCH):
                    act.wait_ge(sem("mla_ps"), c + 1)
                    nc.scalar.activation(xT[:, CH * c:CH * (c + 1)], bank[2 + c % 2][:], ACT.Identity,
                                         bias=w_sb["bo2"][:, 0:1]).then_inc(sem("mla"), 1)

            def deviation(k, g, chunks):
                group = slice(TPC * chunks[0], TPC * (chunks[-1] + 1))
                act.wait_ge(sem("var"), 2 * (k - 1) + g + 1)
                nc.scalar.activation(std[:, group], std[:, group], ACT.Sqrt).then_inc(sem("std"), 1)

            def experts(f):
                def routing():
                    act.wait_ge(sem(f"route_in_{f}"), 1)
                    if f == 0:
                        nc.scalar.activation(small[:, 0, :], small[:, 0, :], ACT.Exp
                                             ).then_inc(sem(f"route_exp_{f}"), 1)
                    else:
                        nc.scalar.activation(logits[:], logits[:], ACT.Exp).then_inc(sem(f"route_exp_{f}"), 1)

                def gates():
                    for c in range(NCH):
                        act.wait_ge(sem(f"gateT_ps_{f}"), c + 1)
                        nc.scalar.activation(gateT[:, CH * c:CH * (c + 1)], bank[6 + c % 2][0:E, :], ACT.Copy
                                             ).then_inc(sem(f"gateT_{f}"), 1)

                for m in range(NCH * E):
                    if m == (2, 0)[f]:
                        routing()
                    if m == 3:
                        gates()
                    if m == E * LAST_APART[1][0] + 4:
                        deviation(2 * f + 2, 0, LAST_APART[0])
                    act.wait_ge(sem(f"hid_ps_{f}"), m + 1)
                    if m >= 2:
                        act.wait_ge(sem(f"y_ps_{f}"), m - 1)
                    for fb in range(FB):
                        e = m % E
                        nc.scalar.activation(hidden[:, m % 2, fb, :], bank[2 * (m % 2) + fb][:],
                                             ACT.Relu if f == 0 else ACT.Gelu,
                                             bias=w_sb[f"b1_{f}"][:, FB * e + fb:FB * e + fb + 1]
                                             ).then_inc(sem(f"hid_{f}"), 1)

            loaded(act, "attn0")
            transposed(0, BY_SEQUENCE[0])
            qkv(ATTENTIONS[0], 0)
            effective_weights()
            attention(ATTENTIONS[0])
            projected(ATTENTIONS[0])
            for g, chunks in enumerate(BY_SEQUENCE):
                deviation(1, g, chunks)
                transposed(1, chunks)
            loaded(act, "ffn0")
            experts(0)
            transposed(2, BY_SEQUENCE[0])
            deviation(2, 1, LAST_APART[1])
            qkv(ATTENTIONS[1], 2)
            attention(ATTENTIONS[1])
            projected(ATTENTIONS[1])
            deviation(3, 0, BY_SEQUENCE[0])
            transposed(3, BY_SEQUENCE[0])
            deviation(3, 1, BY_SEQUENCE[1])
            loaded(act, "attn2")
            qkv(ATTENTIONS[2], 3)
            attention(ATTENTIONS[2])
            projected(ATTENTIONS[2])
            mla()
            loaded(act, "ffn1")
            experts(1)
            deviation(4, 1, LAST_APART[1])

        @block.vector
        def _(dve):
            linked = [0]

            def link(ins):
                linked[0] += 1
                ins.then_inc(sem("vector_chain"), 1)
                dve.wait_ge(sem("vector_chain"), linked[0])

            def v_out(a, c):
                L = a.layer
                dve.wait_ge(sem(f"v_ps_{L}"), c + 1)
                bv = qkv_weights(a)[3]
                for t in range(TPC):
                    tile = TPC * c + t
                    ins = nc.vector.tensor_tensor(
                        v_of(a)[:, H * (tile // TB):H * (tile // TB + 1), tile % TB, 1:a.dv],
                        bank[4 + c % 2][:, P * t:P * t + a.width].rearrange("p (h d) -> p h d", h=H),
                        bv[:].rearrange("p (h d) -> p h d", h=H), ALU.add)
                ins.then_inc(sem(f"v_all_{L}"), 1)

            def qkv(a):
                L = a.layer
                wd = a.width
                items = [(b, w, c) for b in range(B) for w in range(2) for c in range(NCH // B)]

                if L == 0:
                    dve.wait_ge(sem("constants"), CONSTANTS)
                for m, (b, w, c) in enumerate(items):
                    t = slice(S * b + CH * c, S * b + CH * (c + 1))
                    dve.wait_ge(sem(f"part1_{L}"), 2 * m + 2)
                    if m >= 2:
                        dve.wait_ge(sem(f"part3_{L}"), m - 1)
                    nc.vector.tensor_tensor(rest[0:wd, m % 2, :], whole[0:wd, m % 2, :], parts[w][0:wd, 0, t],
                                            ALU.subtract).then_inc(sem(f"rest_{L}"), 1)
                    if m % 2 == 1:
                        v_out(a, m // 2)

            def attention(a):
                L = a.layer
                C = a.chunks

                def find_max(turn, slot, c):
                    n = RING * turn + slot
                    s1 = S1[a.bank_of[c]]
                    dve.wait_ge(sem(f"scores_q_{L}"), C * n + c + 1)
                    if c == 0:
                        ge(dve, f"neg_max_{L}", n - 3)
                    if a.query_diagonal(c):
                        ins = nc.vector.tensor_reduce(tile_max[:, slot, 4 * c:4 * c + 4, 0],
                                                      s1[:].rearrange("p (t k) -> p t k", k=P), AX.X, ALU.max)
                    else:
                        at = 0
                        for i, first, count in a.by_query[c]:
                            which = (1 if a.causal else 0) + first // 4
                            ins = nc.vector.tensor_reduce(tile_max[:, slot, i, which:which + 1],
                                                          s1[:, at:at + P * count], AX.X, ALU.max)
                            at += P * count
                    ins.then_inc(sem(f"max_taken_{L}"), 1)

                def combine_max(turn, slot):
                    n = RING * turn + slot
                    dve.wait_ge(sem(f"max_taken_{L}"), C * (n + 1))
                    ge(dve, f"neg_parts_{L}", 4 * (n - 3))
                    nc.vector.tensor_reduce(neg_max[:, slot, :], tile_max[:, slot, :, 0:a.maxima], AX.X, ALU.max,
                                            negate=True).then_inc(sem(f"neg_max_{L}"), 1)

                def normalise(n, parity):
                    o = total[:, parity, :, 0:a.dv]
                    dve.wait_ge(sem(f"total_{L}"), a.adds * (n + 1))
                    nc.vector.reciprocal(den_inv[:, parity, :], o[:, :, 0]).then_inc(sem(f"normalised_{L}"), 1)
                    dve.wait_ge(sem(f"normalised_{L}"), 2 * n + 1)
                    nc.vector.tensor_tensor(
                        heads_out[:, bass.ds(n * (TB * a.hd), TB * a.hd)].rearrange("p (t d) -> p t d", d=a.hd),
                        o[:, :, 1:a.dv], den_inv[:, parity, :].unsqueeze(2).to_broadcast([P, TB, a.hd]), ALU.mult
                        ).then_inc(sem(f"normalised_{L}"), 1)

                for n in range(AHEAD):
                    for c in range(C):
                        find_max(0, n, c)
                    combine_max(0, n)

                def head(turn, slot):
                    n = RING * turn + slot
                    for k, batch in enumerate(a.batches):
                        if not is_last(turn, slot, AHEAD):
                            for c in batch:
                                find_max(turn + (slot + AHEAD) // RING, (slot + AHEAD) % RING, c)
                    if not is_last(turn, slot, AHEAD):
                        combine_max(turn + (slot + AHEAD) // RING, (slot + AHEAD) % RING)
                    if not is_first(n):
                        normalise(n - 1, (slot + 1) % 2)

                over_heads(dve, head)
                normalise(NH - 1, (NH - 1) % 2)

            def layer_norm(k, g, chunks, chunk_sum):
                for c in chunks:
                    chunk_sum(c)
                tiles = range(TPC * chunks[0], TPC * (chunks[-1] + 1))
                group = slice(tiles[0], tiles[-1] + 1)
                for t in tiles:
                    ins = nc.vector.bn_stats(stats[:, t, :], x_plus[:, t, :])
                link(ins)
                for t in tiles:
                    ins = nc.vector.bn_aggr(mean_var[:, t, :], stats[:, t, :])
                link(ins)
                nc.vector.tensor_scalar(std[:, group], mean_var[:, group, 1], LN_EPS, None, ALU.add
                                        ).then_inc(sem("var"), 1)
                dve.wait_ge(sem("std"), 2 * (k - 1) + g + 1)
                link(nc.vector.reciprocal(rstd[:, group], std[:, group]))
                for t in tiles:
                    ins = nc.vector.tensor_scalar(x[:, t, :], x_plus[:, t, :], mean_var[:, t, 0:1], rstd[:, t:t + 1],
                                                  ALU.subtract, ALU.mult)
                    if t % TPC == TPC - 1:
                        ins.then_inc(sem(f"normed_{k}"), 1)

            def after_attention(a):
                L = a.layer

                def chunk_sum(c):
                    t = slice(TPC * c, TPC * (c + 1))
                    dve.wait_ge(sem(f"x_plus_{L}"), c + 1)
                    dve.wait_ge(sem(f"o_ps_{L}"), c + 1)
                    nc.vector.tensor_tensor(x_plus[:, t, :], bank[2 + c % 2][:].rearrange("p (t d) -> p t d", d=D),
                                            x_plus[:, t, :], ALU.add).then_inc(sem(f"summed_{L}"), 1)
                    dve.wait_ge(sem(f"summed_{L}"), c + 1)

                for g, chunks in enumerate(BY_SEQUENCE):
                    layer_norm(2 * L + 1, g, chunks, chunk_sum)

            def bcast(ap):
                return ap.unsqueeze(2).to_broadcast([P, NT, E])

            def experts(f):
                loaded(dve, f"ffn{f}")
                dve.wait_ge(sem(f"logits_ps_{f}"), 1)
                link(nc.vector.tensor_tensor(logits[:], bank[6][:, 0:NT * E].rearrange("p (t e) -> p t e", e=E),
                                             w_sb[f"br_{f}"][:].unsqueeze(1).to_broadcast([P, NT, E]), ALU.add))
                w1, w2, tmp, inv = (small[:, i, :] for i in (1, 2, 3, 4))
                if f == 1:
                    link(nc.vector.tensor_reduce(tmp, logits[:], AX.X, ALU.max))
                    nc.vector.tensor_tensor(logits[:], logits[:], bcast(tmp), ALU.subtract
                                            ).then_inc(sem(f"route_in_{f}"), 1)
                    dve.wait_ge(sem(f"route_exp_{f}"), 1)
                    link(nc.vector.reduce_sum(tmp, logits[:], AX.X))
                    link(nc.vector.reciprocal(inv, tmp))
                    link(nc.vector.tensor_tensor(logits[:], logits[:], bcast(inv), ALU.mult))
                for t in range(NT):
                    ins = nc.vector.max(top[:, t, :], logits[:, t, :])
                link(ins)
                for t in range(NT):
                    ins = nc.vector.max_index(top_at[:, t, :], top[:, t, :], logits[:, t, :])
                link(ins)
                if f == 0:
                    nc.vector.tensor_tensor(small[:, 0, :], top[:, :, 1], top[:, :, 0], ALU.subtract
                                            ).then_inc(sem(f"route_in_{f}"), 1)
                    dve.wait_ge(sem(f"route_exp_{f}"), 1)
                    link(nc.vector.tensor_scalar(tmp, small[:, 0, :], 1.0, None, ALU.add))
                    link(nc.vector.reciprocal(w1, tmp))
                    link(nc.vector.tensor_tensor(w2, small[:, 0, :], w1, ALU.mult))
                else:
                    link(nc.vector.tensor_tensor(tmp, top[:, :, 0], top[:, :, 1], ALU.add))
                    link(nc.vector.tensor_scalar(tmp, tmp, 1e-8, None, ALU.add))
                    link(nc.vector.reciprocal(inv, tmp))
                    link(nc.vector.tensor_tensor(w1, top[:, :, 0], inv, ALU.mult))
                    link(nc.vector.tensor_tensor(w2, top[:, :, 1], inv, ALU.mult))
                link(nc.vector.tensor_copy(top_f[:], top_at[:, :, 0:2]))
                for i, w in enumerate((w1, w2)):
                    link(nc.vector.tensor_tensor(pick[:, i], iota[:].unsqueeze(1).to_broadcast([P, NT, E]),
                                                 bcast(top_f[:, :, i]), ALU.is_equal))
                    link(nc.vector.tensor_tensor(pick[:, i], pick[:, i], bcast(w), ALU.mult))
                nc.vector.tensor_tensor(gate[:], pick[:, 0], pick[:, 1], ALU.add).then_inc(sem(f"gate_{f}"), 1)
                dve.wait_ge(sem(f"gate_{f}"), 1)
                for c in range(NCH):
                    dve.wait_ge(sem(f"gb_ps_{f}"), c + 1)
                    nc.vector.tensor_copy(acc[:, TPC * c:TPC * (c + 1), :],
                                          bank[6 + c % 2][:].rearrange("p (t d) -> p t d", d=D)
                                          ).then_inc(sem(f"gb_{f}"), 1)
                dve.wait_ge(sem(f"gb_{f}"), NCH)
                def chunk_sum(c):
                    t = slice(TPC * c, TPC * (c + 1))
                    dve.wait_ge(sem(f"y_taken_{f}"), E * (c + 1))
                    if f == 0:
                        link(nc.vector.tensor_tensor(x_plus[:, t, :], x[:, t, :], acc[:, t, :], ALU.add))
                    else:
                        xt = x[:, t, :].rearrange("p t d -> p (t d)")
                        xp = x_plus[:, t, :].rearrange("p t d -> p (t d)")
                        link(nc.vector.scalar_tensor_tensor(xp, acc[:, t, :].rearrange("p t d -> p (t d)"), MIX, xt,
                                                            ALU.mult, ALU.add))
                        link(nc.vector.tensor_tensor(xp, xp, xt, ALU.add))

                for m in range(NCH * E):
                    c, e = m // E, m % E
                    if m == E * LAST_APART[1][0] + 2:
                        layer_norm(2 * f + 2, 0, LAST_APART[0], chunk_sum)
                    dve.wait_ge(sem(f"y_ps_{f}"), m + 1)
                    ge(dve, f"y_taken_{f}", m)
                    for t in range(TPC):
                        tile = TPC * c + t
                        ins = nc.vector.scalar_tensor_tensor(acc[:, tile, :], bank[4 + m % 2][:, P * t:P * (t + 1)],
                                                             gate[:, tile, e:e + 1], acc[:, tile, :],
                                                             ALU.mult, ALU.add)
                    ins.then_inc(sem(f"y_taken_{f}"), 1)

                layer_norm(2 * f + 2, 1, LAST_APART[1], chunk_sum)

            loaded(dve, "attn0")
            qkv(ATTENTIONS[0])
            attention(ATTENTIONS[0])
            after_attention(ATTENTIONS[0])
            experts(0)
            loaded(dve, "attn1")
            qkv(ATTENTIONS[1])
            attention(ATTENTIONS[1])
            after_attention(ATTENTIONS[1])
            loaded(dve, "attn2")
            qkv(ATTENTIONS[2])
            attention(ATTENTIONS[2])
            experts(1)

        @block.tensor
        def _(pe):
            mm = nc.tensor.matmul

            def transpose_x(k, chunks):
                for c in chunks:
                    if k == 0:
                        pe.wait_ge(sem("loaded_x"), 16 * NCH)
                    else:
                        pe.wait_ge(sem(f"normed_{k}"), c + 1)
                    if c >= 2:
                        pe.wait_ge(sem(f"xT_{k}"), c - 1)
                    for t in range(TPC):
                        ins = nc.tensor.transpose(bank[c % 2][:, P * t:P * (t + 1)], x[:, TPC * c + t, :], ident[:])
                    ins.then_inc(sem(f"xT_ps_{k}"), 1)

            def effective_weights():
                loaded(pe, "low_rank")
                for w, (a_n, b_n) in enumerate((("q_aT", "q_b"), ("k_aT", "k_b"))):
                    for h in range(H):
                        ins = mm(bank[6 + w][:, 8 * h:8 * h + 8], w_sb[a_n][:, h, :], w_sb[b_n][:, h, :],
                                 start=True, stop=True)
                    ins.then_inc(sem("w_eff_ps"), 1)
                pe.wait_ge(sem("w_eff"), 2)

            def qkv(a, k):
                L = a.layer
                wd = a.width
                wq, wk, wv, *_ = qkv_weights(a)
                items = [(b, w, c) for b in range(B) for w in range(2) for c in range(NCH // B)]
                for m, (b, w, c) in enumerate(items):
                    if m % (len(items) // B) == 0:
                        transpose_x(k, BY_SEQUENCE[b])
                        pe.wait_ge(sem(f"xT_{k}"), (b + 1) * (NCH // B))
                    if m == 0 and L > 0:
                        pe.wait_ge(*((sem("y_taken_0"), NCH * E) if L == 1 else (sem("summed_1"), NCH)))
                    if m >= 2:
                        pe.wait_ge(sem(f"part1_{L}"), 2 * (m - 1))
                    mm(bank[2 + m % 2][0:wd, :], (wq, wk)[w], xT[:, S * b + CH * c:S * b + CH * (c + 1)],
                       start=True, stop=True).then_inc(sem(f"qk_ps_{L}"), 1)
                    if m % 2 == 1:
                        cv = m // 2
                        ge(pe, f"v_all_{L}", cv - 1)
                        for t in range(TPC):
                            tile = TPC * cv + t
                            ins = mm(bank[4 + cv % 2][:, P * t:P * t + wd], xT[:, P * tile:P * (tile + 1)], wv,
                                     start=True, stop=True)
                        ins.then_inc(sem(f"v_ps_{L}"), 1)

            def attention(a):
                L = a.layer
                C = a.chunks
                K, KM = a.rows, a.rows_m

                def scores_by_query(turn, slot, c):
                    n = RING * turn + slot
                    s1 = S1[a.bank_of[c]]
                    if c == 0:
                        pe.wait_ge(sem(f"qk_in{slot}"), 16 * 2 * PARTS * (turns_before(L) + turn + 1))
                    ge(pe, f"max_taken_{L}", C * n + c + 1 - a.bank_back[c])
                    first = True
                    if a.query_diagonal(c):
                        mm(s1[:], ident16[:], mask16[:].rearrange("p t k -> p (t k)"), start=True, stop=False,
                           skip_group_check=True)
                        first = False
                    at = 0
                    for i, k0, count in a.by_query[c]:
                        ins = mm(s1[:, at:at + P * count], qx[0:K, slot, P * i:P * (i + 1)],
                                 kx_of(a)[0:K, slot, P * k0:P * (k0 + count)], start=first, stop=True,
                                 skip_group_check=not first)
                        at += P * count
                    ins.then_inc(sem(f"scores_q_{L}"), 1)

                def scores_by_key(turn, slot, c):
                    n = RING * turn + slot
                    s2 = S2[a.bank_of[c]]
                    if c == 0:
                        pe.wait_ge(sem(f"max_in{slot}"), 16 * PARTS * (turns_before(L) + turn + 1))
                    ge(pe, f"probs_{L}", C * n + c + 1 - a.bank_back[c])
                    at = 0
                    for j, q0, count, _ in a.by_key[c]:
                        ins = mm(s2[:, at:at + P * count], kx_of(a)[0:KM, slot, P * j:P * (j + 1)],
                                 qx[0:KM, slot, P * q0:P * (q0 + count)], start=True, stop=True)
                        at += P * count
                    ins.then_inc(sem(f"scores_k_{L}"), 1)

                def max_rows(turn, slot):
                    n = RING * turn + slot
                    pe.wait_ge(sem(f"neg_parts_{L}"), 4 * (n + 1))
                    ge(pe, f"by_quarter_{L}", n - 2)
                    nc.tensor.transpose(neg_ps, neg_parts[:, slot].rearrange("p c t -> p (c t)"), ident16[:]
                                        ).then_inc(sem(f"neg_ps_{L}"), 1)

                order = [(c, b, q0 // 4, quarter) for c in range(C) for b, (_, q0, _, quarter) in enumerate(a.by_key[c])]
                opens = {next(m for m in order if m[2:] == hq) for hq in {m[2:] for m in order}}
                closes = {next(m for m in reversed(order) if m[2:] == hq) for hq in {m[2:] for m in order}}

                def probs_by_v(turn, slot, c):
                    n = RING * turn + slot
                    if c == 0:
                        pe.wait_ge(sem(f"v_head_{L}"), n + 1)
                        ge(pe, f"sums_{L}", n)
                    if c in a.masked:
                        pe.wait_ge(sem(f"masked_{L}"), 2 * n + a.masked.index(c) + 1)
                    else:
                        pe.wait_ge(sem(f"probs_{L}"), C * n + c + 1)
                    at = 0
                    for b, (j, q0, count, quarter) in enumerate(a.by_key[c]):
                        half, q = q0 // 4, P * (q0 % 4)
                        this = (c, b, half, quarter)
                        ins = mm(SUM[Q * quarter:Q * (quarter + 1), q:q + P * count], v_head[:, slot, j, :],
                                 probs[:, (C * slot + c) % a.probs_ring, at:at + P * count],
                                 start=this in opens, stop=this in closes, skip_group_check=True)
                        at += P * count
                    ins.then_inc(sem(f"pv_{L}"), 1)

                def turn_sums(n, parity):
                    pe.wait_ge(sem(f"sums_{L}"), n + 1)
                    ge(pe, f"by_quarter_{L}", n)
                    if not (isinstance(n, int) and n == NH - 1):
                        pe.wait_ge(sem(f"neg_rows_{L}"), min(n + 3, NH) if isinstance(n, int) else n + 3)
                    for i in range(4):
                        ins = nc.tensor.transpose(OUT[:, P * i:P * (i + 1)], sums[:, parity, P * i:P * (i + 1)], ident[:])
                    ins.then_inc(sem(f"out_{L}"), 1)

                for n in range(AHEAD):
                    for c in range(C):
                        if n == 1 and c == C // 2:
                            max_rows(0, 0)
                        scores_by_query(0, n, c)
                scores_by_query(0, AHEAD, 0)

                def head(turn, slot):
                    n = RING * turn + slot
                    for k, batch in enumerate(a.batches):
                        for c in batch:
                            ahead = AHEAD + (c + 1) // C
                            if not is_last(turn, slot, ahead):
                                scores_by_query(turn + (slot + ahead) // RING, (slot + ahead) % RING, (c + 1) % C)
                            scores_by_key(turn, slot, c)
                        if k == 0 and not is_last(turn, slot, 1):
                            max_rows(turn + (slot + 1) // RING, (slot + 1) % RING)
                        if k == 1 and not is_first(n):
                            turn_sums(n - 1, (slot + 1) % 2)
                        if k > 0:
                            for c in a.batches[k - 1]:
                                probs_by_v(turn, slot, c)
                        elif not is_first(n):
                            for c in a.batches[-1]:
                                probs_by_v(turn + (slot + 3) // RING - 1, (slot + 3) % RING, c)

                over_heads(pe, head)
                for c in a.batches[-1]:
                    probs_by_v(NH // RING - 1, RING - 1, c)
                turn_sums(NH - 1, (NH - 1) % 2)

            def transpose_a(a, c):
                for t in range(TPC):
                    pe.wait_ge(sem(f"a_tok_{a.layer}"), TPC * c + t + 1)
                    if t == 0:
                        ge(pe, f"aT_{a.layer}", c - 1)
                    ins = nc.tensor.transpose(bank[c % 2][0:a.width, P * t:P * (t + 1)],
                                              a_tok[:, TPC * c + t, 0:a.width], ident[:])
                ins.then_inc(sem(f"aT_ps_{a.layer}"), 1)

            def project(a):
                L = a.layer
                transpose_a(a, 0)
                for c in range(NCH):
                    if c + 1 < NCH:
                        transpose_a(a, c + 1)
                    pe.wait_ge(sem(f"aT_{L}"), c + 1)
                    if c >= 2:
                        pe.wait_ge(sem(f"summed_{L}"), c - 1)
                    for t in range(TPC):
                        tile = TPC * c + t
                        ins = mm(bank[2 + c % 2][:, P * t:P * (t + 1)], aT[:, P * tile:P * (tile + 1)],
                                 w_sb[f"woT{L}"][:], start=True, stop=True)
                    ins.then_inc(sem(f"o_ps_{L}"), 1)

            def project_mla(a):
                transpose_a(a, 0)
                for c in range(NCH):
                    if c + 1 < NCH:
                        transpose_a(a, c + 1)
                    pe.wait_ge(sem(f"aT_{a.layer}"), c + 1)
                    ge(pe, "mla", c - 1)
                    mm(bank[2 + c % 2][:], w_sb["wo2"][:], aT[0:a.width, CH * c:CH * (c + 1)], start=True, stop=True
                       ).then_inc(sem("mla_ps"), 1)

            def experts(f):
                loaded(pe, f"ffn{f}")
                pe.wait_ge(sem("xT_1" if f == 0 else "mla"), NCH)
                for t in range(NT):
                    ins = mm(bank[6][:, E * t:E * (t + 1)], xT[:, P * t:P * (t + 1)], w_sb[f"wr_{f}"][:],
                             start=True, stop=True)
                ins.then_inc(sem(f"logits_ps_{f}"), 1)

                def up(m):
                    c, e = m // E, m % E
                    ge(pe, f"hid_{f}", 2 * (m - 1))
                    for fb in range(FB):
                        ins = mm(bank[2 * (m % 2) + fb][:], w_sb[f"w1_{f}"][:, e, P * fb:P * (fb + 1)],
                                 xT[:, CH * c:CH * (c + 1)], start=True, stop=True)
                    ins.then_inc(sem(f"hid_ps_{f}"), 1)

                def down(m):
                    e = m % E
                    ge(pe, f"y_taken_{f}", m - 1)
                    pe.wait_ge(sem(f"hid_{f}"), 2 * (m + 1))
                    for t in range(TPC):
                        for fb in range(FB):
                            ins = mm(bank[4 + m % 2][:, P * t:P * (t + 1)], hidden[:, m % 2, fb, P * t:P * (t + 1)],
                                     w_sb[f"w2_{f}"][:, e, fb, :], start=fb == 0, stop=fb == FB - 1)
                    ins.then_inc(sem(f"y_ps_{f}"), 1)

                def gates():
                    pe.wait_ge(sem(f"gate_{f}"), 1)
                    for two in range(0, NCH, 2):
                        for c in (two, two + 1):
                            ge(pe, f"gb_{f}", c - 1)
                            for t in range(TPC):
                                ins = nc.tensor.transpose(bank[6 + c % 2][0:E, P * t:P * (t + 1)],
                                                          gate[:, TPC * c + t, :], ident[:])
                            ins.then_inc(sem(f"gateT_ps_{f}"), 1)
                        if two == 0:
                            up(3)
                        for c in (two, two + 1):
                            pe.wait_ge(sem(f"gateT_{f}"), c + 1)
                            for t in range(TPC):
                                tile = TPC * c + t
                                ins = mm(bank[6 + c % 2][:, P * t:P * (t + 1)], gateT[:, P * tile:P * (tile + 1)],
                                         w_sb[f"b2_{f}"][:], start=True, stop=True)
                            ins.then_inc(sem(f"gb_ps_{f}"), 1)

                up(0)
                for m in range(NCH * E):
                    if m + 1 < NCH * E and m != 2:
                        up(m + 1)
                    down(m)
                    if m == 1:
                        gates()

            pe.wait_ge(sem("constants"), CONSTANTS)
            loaded(pe, "attn0")
            qkv(ATTENTIONS[0], 0)
            effective_weights()
            attention(ATTENTIONS[0])
            project(ATTENTIONS[0])
            transpose_x(1, range(NCH))
            experts(0)
            loaded(pe, "attn1")
            qkv(ATTENTIONS[1], 2)
            attention(ATTENTIONS[1])
            project(ATTENTIONS[1])
            loaded(pe, "attn2")
            qkv(ATTENTIONS[2], 3)
            attention(ATTENTIONS[2])
            project_mla(ATTENTIONS[2])
            experts(1)


CONSTANTS = 14


def kernel(**inputs):
    import numpy as np
    import concourse.bacc as bacc
    from concourse import mybir as _mybir
    from concourse.bass_utils import run_bass_kernel_spmd

    g = {n: np.asarray(v) for n, v in inputs.items()}
    f32 = np.float32
    nc = bacc.Bacc("TRN2", target_bir_lowering=False, num_devices=1)
    arrays, inp = {}, {}

    def give(name, a, group):
        a = np.ascontiguousarray(a)
        arrays["in_" + name] = a
        inp[name] = (nc.dram_tensor("in_" + name, a.shape, _mybir.dt.from_np(a.dtype), kind="ExternalInput").ap(), group)

    def over_tokens(row):
        return np.broadcast_to(row.reshape(1, -1), (P, row.size))

    give("x", g["L0_attn_x"].reshape(T, D), "x")
    give("wqT0", g["L0_attn_Wq"].T, "attn0")
    give("wkT0", g["L0_attn_Wk"].T, "attn0")
    give("wvT0", g["L0_attn_Wv"].T, "attn0")
    give("woT0", g["L0_attn_Wo"].T, "attn0")
    give("bq0", g["L0_attn_bq"].reshape(D, 1), "attn0")
    give("bk0", g["L0_attn_bk"].reshape(D, 1), "attn0")
    give("bv0", over_tokens(g["L0_attn_bv"]), "attn0")
    give("bo0", over_tokens(g["L0_attn_bo"]), "attn0")
    give("q_aT", g["L1_attn_q_a"].transpose(2, 0, 1), "low_rank")
    give("q_b", g["L1_attn_q_b"].transpose(1, 0, 2), "low_rank")
    give("k_aT", g["L1_attn_k_a"].transpose(2, 0, 1), "low_rank")
    give("k_b", g["L1_attn_k_b"].transpose(1, 0, 2), "low_rank")

    def experts(f, wr, br, w1, b1, w2, b2):
        give(f"wr_{f}", g[wr], f"ffn{f}")
        give(f"br_{f}", over_tokens(g[br]), f"ffn{f}")
        give(f"w1_{f}", g[w1].transpose(1, 0, 2), f"ffn{f}")
        give(f"b1_{f}", g[b1].reshape(E * FB, P).T, f"ffn{f}")
        give(f"w2_{f}", g[w2].reshape(E, FB, P, D).transpose(2, 0, 1, 3), f"ffn{f}")
        give(f"b2_{f}", g[b2], f"ffn{f}")

    experts(0, "L0_ffn_Wr", "L0_ffn_br", "L0_ffn_W1", "L0_ffn_b1", "L0_ffn_W2", "L0_ffn_b2")
    give("wvT1", g["L1_attn_v_w"].T, "attn1")
    give("woT1", g["L1_attn_o_w"].T, "attn1")
    give("bv1", over_tokens(g["L1_attn_v_b"]), "attn1")
    give("bo1", over_tokens(g["L1_attn_o_b"]), "attn1")
    lat = D // 2
    kph = lat // H
    give("wq2", g["L1_ffn_q_w"].reshape(D, H, D // H)[:, :, :kph].reshape(D, lat), "attn2")
    give("wk2", g["L1_ffn_k_w"], "attn2")
    give("wv2", g["L1_ffn_v_w"], "attn2")
    give("wo2", g["L1_ffn_o_w"][:lat], "attn2")
    give("bq2", g["L1_ffn_q_b"].reshape(H, D // H)[:, :kph].reshape(lat, 1), "attn2")
    give("bk2", g["L1_ffn_k_b"].reshape(lat, 1), "attn2")
    give("bv2", over_tokens(g["L1_ffn_v_b"]), "attn2")
    give("bo2", g["L1_ffn_o_b"].reshape(D, 1), "attn2")
    experts(1, "L1_ffn_router_w", "L1_ffn_router_b", "L1_ffn_w1", "L1_ffn_b1", "L1_ffn_w2", "L1_ffn_b2")

    out = nc.dram_tensor("out_x", (T, D), F32, kind="ExternalOutput").ap()
    build(nc, inp, out)
    r = run_bass_kernel_spmd(nc, [arrays], core_ids=[0])
    return r.results[0]["out_x"].reshape(B, S, D)
```
